# Optimizing a Trainium2 kernel written in Bass

```python
import numpy as np
import jax
import jax.numpy as jnp

def _softmax(x, axis=-1):
    return jax.nn.softmax(x, axis=axis)

def _gelu(x):
    return jax.nn.gelu(x, approximate=True)

def _silu(x):
    return jax.nn.silu(x)

def _sigmoid(x):
    return jax.nn.sigmoid(x)

def _layernorm(x, axis=-1, eps=1e-05):
    m = jnp.mean(x, axis=axis, keepdims=True)
    v = jnp.var(x, axis=axis, keepdims=True)
    return (x - m) / jnp.sqrt(v + eps)

def _scatter_add(tgt, idx, src, axis=0):
    return tgt.at[idx].add(src)

def _segment_sum(src, seg, n):
    return jax.ops.segment_sum(src, seg, n)
kernel_name = 'mk_gnn_resnorm_d1_gnn_r8_fc685f'

def setup_inputs(seed: int=0):
    np.random.seed(seed)
    _w = jnp.asarray

    def _rec_inputs():
        import jax
        import jax.numpy as jnp
        _gk = jax.random.key(seed)
        x = -8.776e-05 + 1 * jax.random.normal(jax.random.fold_in(_gk, 1), (6250, 512), jnp.float32)
        src = jax.random.randint(jax.random.fold_in(_gk, 2), (100000,), 0, 6250, jnp.int32)
        dst = jax.random.randint(jax.random.fold_in(_gk, 3), (100000,), 0, 6250, jnp.int32)
        _o = jnp.argsort(dst, stable=True)
        src = src[_o]
        dst = dst[_o]
        return (x, src, dst)
    x, src, dst = _rec_inputs()

    def _L0_gnn_setup():
        import jax, jax.numpy as jnp
        import numpy as np
        N_NODES = 1250
        N_EDGES = 20000
        D_IN = 512
        D_HID = 1024
        key = jax.random.key(seed)
        ks = jax.random.split(key, 8)
        feat = jax.random.normal(ks[0], (N_NODES, D_IN), dtype=jnp.float32)
        W1 = jax.random.normal(ks[1], (D_IN, D_HID), dtype=jnp.float32) * (1.0 / np.sqrt(D_IN))
        b1 = jnp.zeros((D_HID,), dtype=jnp.float32)
        W2 = jax.random.normal(ks[2], (D_HID, D_IN), dtype=jnp.float32) * (1.0 / np.sqrt(D_HID))
        b2 = jnp.zeros((D_IN,), dtype=jnp.float32)
        eps = jnp.zeros((1,), dtype=jnp.float32)
        src = jax.random.randint(ks[3], (N_EDGES,), 0, N_NODES, dtype=jnp.int32)
        dst = jax.random.randint(ks[4], (N_EDGES,), 0, N_NODES, dtype=jnp.int32)
        return {'feat': feat, 'W1': W1, 'b1': b1, 'W2': W2, 'b2': b2, 'eps': eps, 'src': src, 'dst': dst}
    _L0_gnn_all = _L0_gnn_setup()
    _L0_gnn_in = {k: v for k, v in _L0_gnn_all.items() if k in ('W1', 'b1', 'W2', 'b2', 'eps')}
    del _L0_gnn_all
    return {'x': x, 'src': src, 'dst': dst, 'L0_gnn_W1': _L0_gnn_in['W1'], 'L0_gnn_b1': _L0_gnn_in['b1'], 'L0_gnn_W2': _L0_gnn_in['W2'], 'L0_gnn_b2': _L0_gnn_in['b2'], 'L0_gnn_eps': _L0_gnn_in['eps']}

def reference(x, src, dst, L0_gnn_W1, L0_gnn_b1, L0_gnn_W2, L0_gnn_b2, L0_gnn_eps):
    import jax
    import jax.numpy as jnp

    def _L0_gnn_ref(feat, W1, b1, W2, b2, eps, src, dst):
        import jax, jax.numpy as jnp
        import numpy as np
        N_NODES = 1250
        N_EDGES = 20000
        D_IN = 512
        D_HID = 1024
        msgs = feat[src]
        neigh = jax.ops.segment_sum(msgs, dst, num_segments=feat.shape[0])
        rst = (1.0 + eps[0]) * feat + neigh
        h = jnp.maximum(rst @ W1 + b1, 0.0)
        h = h @ W2 + b2
        return h + feat
    x = _layernorm(x + _L0_gnn_ref(x, L0_gnn_W1, L0_gnn_b1, L0_gnn_W2, L0_gnn_b2, L0_gnn_eps, src, dst), axis=-1)
    return x

_drawn_inputs = setup_inputs


def setup_inputs(seed=0):
    import zlib

    import numpy as np

    out = dict(_drawn_inputs(seed))
    spreads = {'L0_gnn_b1': (0.0, 0.392), 'L0_gnn_b2': (0.0, 0.27)}
    factors = {}
    for name, (base, spread) in spreads.items():
        noise = np.random.default_rng([zlib.crc32(name.encode()), seed]).standard_normal(out[name].shape)
        drawn = base * np.exp(spread * noise) if base else spread * noise
        out[name] = jnp.asarray(drawn.astype(out[name].dtype))
    for name, factor in factors.items():
        out[name] = (out[name] * factor).astype(out[name].dtype)
    return out
```

```python
from contextlib import ExitStack

import concourse.bass as bass
from concourse import mybir

F32 = mybir.dt.float32
F32R = mybir.dt.float32r
I32 = mybir.dt.int32
ALU = mybir.AluOpType
ACT = mybir.ActivationFunctionType
AX = mybir.AxisListType

P = 128
N = 6250
E = 100000
D = 512
HID = 1024
TN = 125
TILES = N // TN
GROUPS = TILES // 2
SLOTS = 17
WIN = SLOTS * P
STEPS = 2 * SLOTS
RING = 4
AHEAD = 3
TC = D // P
HC = HID // P
PAIRS = HC // 2
ROW = 160
RP = 125
BLK = E // (ROW * RP)
GT = 125
GTILES = E // GT
WPIECES = 8
LN_EPS = 1e-5
FAR = 1.0e6
assert TN * TILES == N and ROW * RP * BLK == E and GT * GTILES == E

STEP_WINDOW_F32 = 1
STEP_WINDOW_T = 2
STEP_RST = 3
STEP_TABLES = 5
STEP_RST_T = 6
STEP_ONEHOT = 8
STEP_RST_HI = 10
STEP_RST_LO = 11
OUT_STEPS = 13
Z_STEP = (9, 15)
SQRT_STEP = (12, 18)
NORM_STEP = (15, 21)
RELU_STEP = (19, 24, 29, 34)
HLO_STEP = (20, 25, 30, 35)


def build(nc, x, src, dst, W1, b1, W2, b2, eps, out):
    neigh = nc.dram_tensor("neigh", (N, D), F32, kind="Internal").ap()
    one_src = nc.dram_tensor("one_src", (TILES + AHEAD, WIN), I32, kind="Internal").ap()
    one_dst = nc.dram_tensor("one_dst", (TILES + AHEAD, WIN), I32, kind="Internal").ap()

    with ExitStack() as ctx:
        def sb(name, shape, dt):
            return ctx.enter_context(nc.sbuf_tensor(name, shape, dt))

        def pb(name, shape):
            return ctx.enter_context(nc.psum_tensor(name, shape, F32))

        def sem(name):
            return ctx.enter_context(nc.semaphore(name))

        w1 = [sb(f"w1_{s}", [P, TC, HID], F32R) for s in ("hi", "lo")]
        w2 = [sb(f"w2_{s}", [P, HC, D], F32R) for s in ("hi", "lo")]
        wstage = sb("wstage", [P, 2, HID], F32)
        raw = sb("raw", [P, SLOTS, D], F32)
        msg = [sb(f"msg_{s}", [P, RING, D], F32R) for s in ("hi", "lo")]
        onehot = sb("onehot", [P, 2, SLOTS, TN], F32R)
        xt = sb("xt", [P, 4, D], F32)
        rst = sb("rst", [P, 2, D], F32)
        rstT = [sb(f"rstT_{s}", [P, 2, TC, 2 * TN], F32R) for s in ("hi", "lo")]
        hfull = sb("hfull", [P, 2, 2, 2 * TN], F32)
        hT = [sb(f"hT_{s}", [P, HC, 2 * TN], F32R) for s in ("hi", "lo")]
        z = sb("z", [P, 2, D], F32)
        b2b = sb("b2b", [P, D], F32)
        b1c = sb("b1c", [P, HC], F32)
        onepe = sb("onepe", [P, 2], F32)
        epsln = sb("epsln", [P, 1], F32)
        ident = sb("ident", [P, P], F32)
        iota_row = sb("iota_row", [P, P], F32)
        iota_col = sb("iota_col", [P, 1], F32)
        first_node = sb("first_node", [P, TILES + AHEAD], F32)
        first_node_col = sb("first_node_col", [P, 1], F32)
        ones = sb("ones", [P, 1], F32)
        win = sb("win", [P, 4, 2, P], I32)
        winf = sb("winf", [P, 2, P], F32)
        idx = sb("idx", [P, 4, SLOTS], I32)
        place = sb("place", [P, 4, SLOTS], F32)
        moments = sb("moments", [P, 2, 6], F32)
        meanvar = sb("meanvar", [P, 2, 2], F32)
        std = sb("std", [P, 2], F32)
        rstd = sb("rstd", [P, 2], F32)
        below = sb("below", [P, BLK, TILES], F32)
        lastf = sb("lastf", [P, BLK], F32)
        boundary = sb("boundary", [P, 4], F32)
        rowidx = sb("rowidx", [P, 1], I32)
        rowdst = sb("rowdst", [P, ROW], I32)
        rowcmp = sb("rowcmp", [P, ROW], F32)
        runs = sb("runs", [1, TILES + 1], F32)
        startf = sb("startf", [1, TILES + AHEAD], F32)
        start = sb("start", [1, TILES + AHEAD], I32)
        runlen = sb("runlen", [1, TILES], F32)
        verdict = sb("verdict", [P, 8], F32)
        flag = sb("flag", [1, 1], I32)
        before = raw[:, :, :].rearrange("p s d -> p (s d)")
        dsti = before[0:RP, 0:BLK * (ROW + 1)].bitcast(I32).rearrange("p (b j) -> p b j", b=BLK)
        falls = before[0:RP, 1024:1024 + BLK * ROW].rearrange("p (b j) -> p b j", b=BLK)

        acc = [pb(f"acc{i}", [P, D]) for i in range(2)]
        tables = pb("tables", [P, D])
        turned = pb("turned", [P, TC, P])
        hp = [pb(f"hp{i}", [P, 2, 2 * TN]) for i in range(2)]
        y = [pb(f"y{i}", [P, D]) for i in range(2)]

        s_iota = sem("s_iota")
        s_const = sem("s_const")
        s_small = sem("s_small")
        s_dst = sem("s_dst")
        s_prep = sem("s_prep")
        s_prep_pe = sem("s_prep_pe")
        s_rowdst = sem("s_rowdst")
        s_flag = sem("s_flag")
        s_wload = [sem(f"s_wload{i}") for i in range(2)]
        s_whi = sem("s_whi")
        s_wlo = sem("s_wlo")
        s_win = [sem(f"s_win{i}") for i in range(4)]
        s_winf = sem("s_winf")
        s_winT = sem("s_winT")
        s_idx = sem("s_idx")
        s_place = sem("s_place")
        s_onehot = sem("s_onehot")
        s_gather = [sem(f"s_gather{k}") for k in range(SLOTS)]
        s_mhi = sem("s_mhi")
        s_mlo = sem("s_mlo")
        s_seg = sem("s_seg")
        s_x = [sem(f"s_x{i}") for i in range(4)]
        s_rst = sem("s_rst")
        s_turn = sem("s_turn")
        s_rhi = sem("s_rhi")
        s_rlo = sem("s_rlo")
        s_mm1 = sem("s_mm1")
        s_relu = sem("s_relu")
        s_hhi = sem("s_hhi")
        s_hlo = sem("s_hlo")
        s_y = sem("s_y")
        s_z1 = sem("s_z1")
        s_z2 = sem("s_z2")
        s_mom = sem("s_mom")
        s_mv = sem("s_mv")
        s_std = sem("s_std")
        s_rstd = sem("s_rstd")
        s_norm = sem("s_norm")
        s_store = [sem(f"s_store{i}") for i in range(2)]
        g_dve = sem("g_dve")
        g_pool = sem("g_pool")
        g_zero = sem("g_zero")
        g_table = sem("g_table")
        g_edge = sem("g_edge")
        g_got = sem("g_got")
        g_pe = sem("g_pe")
        g_put = sem("g_put")
        g_step = sem("g_step")

        block = ctx.enter_context(nc.Block())

        def wait_apart(eng, signal, value):
            value = value if type(value) is int else eng.to_reg(value)
            eng.wait_ge(s_flag, 1)
            eng.wait_ge(signal, value)

        def run_groups(group):
            for g in range(3):
                group(g, 2 * g % 4, 2 * g // 4)

            def pair(it):
                group(2 * it + 1, 2, it)
                group(2 * it + 2, 0, it + 1)
            return pair

        @block.sync
        def _(sp):
            rows = dst.rearrange("(b q j) -> q b j", b=BLK, q=RP)
            sp.dma_start(dsti[:, :, 0:ROW], rows).then_inc(s_dst, 16)
            nxt = dst.rearrange("(r j) -> r j", j=ROW)
            with nc.allow_non_contiguous_dma(reason="one element of each row of dst"):
                for b in range(BLK):
                    n = RP if b < BLK - 1 else RP - 1
                    sp.dma_start(dsti[0:n, b, ROW:ROW + 1],
                                 nxt[b * RP + 1:b * RP + 1 + n, 0:1]).then_inc(s_dst, 16)
                sp.dma_start(dsti[RP - 1:RP, BLK - 1, ROW:ROW + 1],
                             nxt[BLK * RP - 1:BLK * RP, ROW - 1:ROW]).then_inc(s_dst, 16)
            sp.dma_start(onepe[:, 0:1], eps.partition_broadcast(P)).then_inc(s_small, 16)
            sp.dma_start(b2b[:, :], b2.partition_broadcast(P)).then_inc(s_small, 16)
            with nc.allow_non_contiguous_dma(reason="the bias of the hidden layer, one a partition"):
                sp.dma_start(b1c[:, :], b1.rearrange("(c p) -> p c", p=P)).then_inc(s_small, 16)

            def load_x(t, slot):
                sp.dma_start(xt[0:TN, slot, :], x[bass.ds(t * TN, TN), :]).then_inc(s_x[slot], 16)

            def load_weights(q):
                if q >= 2:
                    sp.wait_ge(s_wlo, q - 1)
                if q < TC:
                    piece = W1[q * P:(q + 1) * P, :]
                    sp.dma_start(wstage[:, q % 2, :], piece).then_inc(s_wload[q % 2], 16)
                else:
                    j = 2 * (q - TC)
                    piece = W2[j * P:(j + 2) * P, :].rearrange("(c p) n -> p c n", p=P)
                    room = wstage[:, q % 2, :].rearrange("p (c n) -> p c n", c=2)
                    sp.dma_start(room, piece).then_inc(s_wload[q % 2], 16)

            for q in range(2):
                load_weights(q)
            for t in range(4):
                load_x(t, t)

            def main(window_of):
                def load_window(t, slot):
                    s_rows, d_rows = window_of(t)
                    sp.dma_start(win[0:SLOTS, slot, 0, :], s_rows).then_inc(s_win[slot], 16)
                    sp.dma_start(win[0:SLOTS, slot, 1, :], d_rows).then_inc(s_win[slot], 16)

                for t in range(AHEAD):
                    load_window(t, t)
                for q in range(2, WPIECES):
                    load_weights(q)

                def group(g, res, lap):
                    T0 = 2 * g
                    for i in range(2):
                        T = T0 + i
                        slot = (res + i + 3) % 4
                        if not (type(T) is int and T == 0):
                            sp.wait_ge(s_winf, T)
                        load_window(T + 3, slot)
                        if i == 0 and not (type(g) is int and g < 2):
                            for F, f in ((T0 - 4, 0), (T0 - 3, 1)):
                                sp.wait_ge(s_z1, F + 1)
                                load_x(F + 4, (res + f) % 4)
                                sp.wait_ge(s_norm, F + 1)
                                store(F, f)

                def store(F, f):
                    sp.dma_start(out[bass.ds(F * TN, TN), :], z[0:TN, f, :]).then_inc(s_store[f], 16)

                pair = run_groups(group)
                with sp.Fori(1, GROUPS // 2) as it:
                    pair(it)
                for F in range(TILES - 4, TILES):
                    sp.wait_ge(s_norm, F + 1)
                    store(F, F % 2)
                for f in range(2):
                    sp.wait_ge(s_store[f], 16 * TILES // 2)
                for slot in range(4):
                    n = len(range(slot, TILES + AHEAD, 4))
                    sp.wait_ge(s_win[slot], 32 * n)

            def window_of_edges(t):
                at = sp.value_load(start[0:1, bass.ds(t, 1)], min_val=0, max_val=E - WIN)
                return tuple(a[bass.ds(at, WIN)].rearrange("(k p) -> k p", p=P) for a in (src, dst))

            def window_of_nodes(t):
                return tuple(a[bass.ds(t, 1), :].rearrange("a (k p) -> (a k) p", p=P)
                             for a in (one_src, one_dst))

            sp.wait_ge(s_flag, 1)
            general = sp.value_load(flag[0:1, 0:1], min_val=0, max_val=1)
            with sp.If(general > 0):
                with nc.allow_non_contiguous_dma(reason="an edge a partition"):
                    with sp.Fori(0, GTILES) as t:
                        sp.wait_ge(g_step, t + 1)
                        sp.dma_start(rowidx[0:GT, :], src[bass.ds(t * GT, GT)].rearrange("(p a) -> p a", a=1)
                                     ).then_inc(g_edge, 16)
                        sp.dma_start(rowdst[0:GT, 0:1], dst[bass.ds(t * GT, GT)].rearrange("(p a) -> p a", a=1)
                                     ).then_inc(g_edge, 16)
                sp.wait_ge(g_table, 32)
                main(window_of_nodes)
            with sp.Else():
                main(window_of_edges)

        @block.gpsimd
        def _(pool):
            pool.iota(iota_row[:, :], [[1, P]], base=0, channel_multiplier=0,
                      allow_small_or_imprecise_dtypes=True).then_inc(s_iota, 1)
            pool.iota(iota_col[:, :], [[0, 1]], base=0, channel_multiplier=1,
                      allow_small_or_imprecise_dtypes=True).then_inc(s_iota, 1)
            pool.iota(first_node[:, :], [[TN, TILES + AHEAD]], base=0, channel_multiplier=0,
                      allow_small_or_imprecise_dtypes=True).then_inc(s_iota, 1)
            pool.iota(first_node_col[:, :], [[0, 1]], base=0, channel_multiplier=TN,
                      allow_small_or_imprecise_dtypes=True).then_inc(s_iota, 1)
            pool.wait_ge(s_prep, PREP_ROWIDX)
            pool.indirect_dma_start(
                out=rowdst[0:TILES, :], out_offset=None, in_=dst.rearrange("(r j) -> r j", j=ROW),
                in_offset=bass.IndirectOffsetOnAxis(ap=rowidx[0:TILES, 0:1], axis=0)).then_inc(s_rowdst, 16)

            def main(table):
                def group(g, res, lap):
                    T0 = 2 * g
                    for i in range(2):
                        T = T0 + i
                        wait_apart(pool, s_idx, T + 1)
                        for k in range(SLOTS):
                            if not (type(T) is int and T == 0):
                                wait_apart(pool, s_mlo, SLOTS * (T - 1) + k + 1)
                            pool.indirect_dma_start(
                                out=raw[:, k, :], out_offset=None, in_=table[:, :],
                                in_offset=bass.IndirectOffsetOnAxis(
                                    ap=idx[:, (res + i) % 4, k:k + 1], axis=0)).then_inc(s_gather[k], 16)

                pair = run_groups(group)
                with pool.Fori(1, GROUPS // 2) as it:
                    pair(it)

            pool.wait_ge(s_flag, 1)
            general = pool.value_load(flag[0:1, 0:1], min_val=0, max_val=1)
            with pool.If(general > 0):
                node = before[0:TILES, 2048:2048 + WIN].bitcast(I32)
                pool.memset(node, 0).then_inc(g_pool, 1)
                pool.wait_ge(g_pool, 1)
                pool.iota(node[:, 0:TN], [[1, TN]], base=0, channel_multiplier=TN).then_inc(g_pool, 1)
                pool.wait_ge(g_pool, 2)
                pool.dma_start(one_src[0:TILES, :], node).then_inc(g_table, 16)
                pool.wait_ge(g_table, 16)
                pool.memset(node[:, TN:WIN], -1000000).then_inc(g_pool, 1)
                pool.wait_ge(g_pool, 3)
                pool.dma_start(one_dst[0:TILES, :], node).then_inc(g_table, 16)
                pool.memset(raw[:, 8, :], 0.0).then_inc(g_pool, 1)
                pool.wait_ge(g_pool, 4)
                pool.wait_ge(g_table, 32)
                for t in (one_src, one_dst):
                    pool.dma_start(t[TILES:TILES + AHEAD, :],
                                   before[0:AHEAD, 8 * D:8 * D + WIN].bitcast(I32)).then_inc(g_zero, 16)
                with pool.Fori(0, TILES) as t:
                    pool.dma_start(neigh[bass.ds(t * TN, TN), :], raw[0:TN, 8, :]).then_inc(g_zero, 16)
                pool.wait_ge(g_zero, 16 * (TILES + 2))
                pool.memset(before[0:1, 0:1], 0.0).then_inc(g_step, 1)
                with pool.Fori(0, GTILES) as t:
                    wait_apart(pool, g_edge, 32 * t + 32)
                    pool.indirect_dma_start(
                        out=raw[0:GT, 0, :], out_offset=None, in_=x[:, :],
                        in_offset=bass.IndirectOffsetOnAxis(ap=rowidx[0:GT, 0:1], axis=0)).then_inc(g_got, 16)
                    pool.indirect_dma_start(
                        out=raw[0:GT, 1, :], out_offset=None, in_=neigh[:, :],
                        in_offset=bass.IndirectOffsetOnAxis(ap=rowdst[0:GT, 0:1], axis=0)).then_inc(g_got, 16)
                    wait_apart(pool, g_dve, 7 * t + 7)
                    pool.indirect_dma_start(
                        out=neigh[:, :], out_offset=bass.IndirectOffsetOnAxis(ap=rowdst[0:GT, 1:2], axis=0),
                        in_=raw[0:GT, 2, :], in_offset=None, bounds_check=N - 1,
                        oob_is_err=False).then_inc(g_put, 16)
                    wait_apart(pool, g_put, 16 * t + 16)
                    pool.memset(before[0:1, 0:1], 0.0).then_inc(g_step, 1)
                main(neigh)
            with pool.Else():
                main(x)

        @block.scalar
        def _(act):
            def cut_weights(q):
                act.wait_ge(s_wload[q % 2], 16 * (q // 2 + 1))
                to = w1[0][:, q, :] if q < TC else \
                    w2[0][:, 2 * (q - TC):2 * (q - TC) + 2, :].rearrange("p c n -> p (c n)")
                act.activation(to, wstage[:, q % 2, :], ACT.Copy).then_inc(s_whi, 1)

            def rst_hi(T, i, half, m_seen, first):
                act.wait_ge(s_turn, T + 1)
                if not first:
                    act.wait_ge(s_mm1, HC * m_seen)
                act.activation(rstT[0][:, half, :, i * TN:(i + 1) * TN], turned[:, :, 0:TN],
                               ACT.Copy).then_inc(s_rhi, 1)

            def relu_pair(m, jp, first):
                act.wait_ge(s_mm1, HC * m + 2 * jp + 2)
                for jj in range(2):
                    j = 2 * jp + jj
                    if not (first and jp < 2):
                        act.wait_ge(s_hlo, PAIRS * m + jp - 1)
                    act.activation(hfull[:, jp % 2, jj, :], hp[jp % 2][:, jj, :], ACT.Relu,
                                   bias=b1c[:, j:j + 1]).then_inc(s_relu, 1)
                act.wait_ge(s_relu, HC * m + 2 * jp + 2)
                if not first:
                    act.wait_ge(s_y, 2 * m)
                act.activation(hT[0][:, 2 * jp:2 * jp + 2, :], hfull[:, jp % 2, :, :],
                               ACT.Copy).then_inc(s_hhi, 1)

            def root(F, f):
                act.wait_ge(s_mv, F + 1)
                act.activation(std[0:TN, f:f + 1], meanvar[0:TN, f, 1:2], ACT.Sqrt,
                               bias=epsln[0:TN, 0:1]).then_inc(s_std, 1)

            def group(g, res, lap):
                T0 = 2 * g
                static = type(g) is int
                half = 0 if res == 0 else 1
                for p in range(STEPS):
                    i, k = p // SLOTS, p % SLOTS
                    T = T0 + i
                    act.wait_ge(s_gather[k], 16 * T + 16)
                    if not (static and SLOTS * T + k < RING):
                        act.wait_ge(s_seg, SLOTS * T + k + 1 - RING)
                    act.activation(msg[0][:, (res + i + k) % RING, :], raw[:, k, :],
                                   ACT.Copy).then_inc(s_mhi, 1)
                    if static and T == 0 and k % 2 == 0 and k // 2 < WPIECES:
                        cut_weights(k // 2)
                    if k == STEP_RST_HI and not (static and T == 0):
                        if i == 0:
                            rst_hi(T - 1, 1, 1 - half, g - 2, static and g < 3)
                        else:
                            rst_hi(T - 1, 0, half, g - 1, static and g < 2)
                    for jp in range(PAIRS):
                        if p == RELU_STEP[jp] and not (static and g < 1):
                            relu_pair(g - 1, jp, static and g == 1)
                        if p == RELU_STEP[jp] - STEPS and not (static and g < 2):
                            relu_pair(g - 2, jp, static and g == 2)
                    for f in range(2):
                        if p == SQRT_STEP[f] and not (static and g < 2):
                            root(T0 - 4 + f, f)

            act.wait_ge(s_small, 48)
            act.wait_ge(s_const, CONSTS)
            pair = run_groups(group)
            with act.Fori(1, GROUPS // 2) as it:
                pair(it)
            last = GROUPS - 1
            relu_pair(last - 1, PAIRS - 1, False)
            rst_hi(TILES - 1, 1, last % 2, last - 1, False)
            for f in range(2):
                root(TILES - 4 + f, f)
            for jp in range(PAIRS):
                relu_pair(last, jp, False)
            for f in range(2):
                root(TILES - 2 + f, f)

        @block.vector
        def _(dve):
            count = [0]

            def link(ins):
                count[0] += 1
                ins.then_inc(s_prep, 1)
                dve.wait_ge(s_prep, count[0])

            dve.memset(ones[:, :], 1.0).then_inc(s_const, 1)
            dve.memset(epsln[:, :], LN_EPS).then_inc(s_const, 1)
            dve.memset(startf[:, :], 0.0).then_inc(s_const, 1)
            dve.memset(runs[:, :], float(E)).then_inc(s_const, 1)
            dve.memset(verdict[:, :], 0.0).then_inc(s_const, 1)
            dve.wait_ge(s_iota, 4)
            dve.tensor_scalar(ident[:, :], iota_row[:, :], iota_col[:, 0:1], None,
                              ALU.is_equal).then_inc(s_const, 1)
            dve.wait_ge(s_dst, 16 * (BLK + 2))
            link(dve.tensor_copy(lastf[0:RP, :], dsti[:, :, ROW - 1]))
            for b in range(BLK):
                link(dve.tensor_scalar(below[0:RP, b, :], first_node[0:RP, 0:TILES], lastf[0:RP, b:b + 1],
                                       None, ALU.is_gt))
            assert count[0] == PREP_BELOW
            dve.wait_ge(s_prep_pe, 1)
            link(dve.tensor_scalar(boundary[0:TILES, 0:1], tables[0:TILES, 0:1], float(BLK * RP - 1), None,
                                   ALU.min))
            link(dve.tensor_copy(rowidx[0:TILES, :], boundary[0:TILES, 0:1]))
            assert count[0] == PREP_ROWIDX
            link(dve.tensor_tensor(falls, dsti[:, :, 0:ROW], dsti[:, :, 1:ROW + 1], ALU.subtract))
            link(dve.tensor_reduce(verdict[0:RP, 0:1], before[0:RP, 1024:1024 + BLK * ROW], AX.X, ALU.max))
            link(dve.tensor_scalar(verdict[0:RP, 1:2], verdict[0:RP, 0:1], 0.0, None, ALU.is_gt))
            dve.wait_ge(s_rowdst, 16)
            link(dve.tensor_scalar(rowcmp[0:TILES, :], rowdst[0:TILES, :], first_node_col[0:TILES, 0:1], None,
                                   ALU.is_lt))
            link(dve.tensor_reduce(boundary[0:TILES, 1:2], rowcmp[0:TILES, :], AX.X, ALU.add))
            link(dve.scalar_tensor_tensor(out=boundary[0:TILES, 2:3], in0=boundary[0:TILES, 0:1],
                                          scalar=float(ROW), in1=boundary[0:TILES, 1:2],
                                          op0=ALU.mult, op1=ALU.add))
            link(dve.tensor_scalar(boundary[0:TILES, 3:4], boundary[0:TILES, 2:3], float(E - WIN), None,
                                   ALU.min))
            assert count[0] == PREP_BOUNDARY
            dve.wait_ge(s_prep_pe, 2)
            link(dve.tensor_copy(runs[0:1, 0:TILES], tables[0:1, 64:64 + TILES]))
            link(dve.tensor_copy(startf[0:1, 0:TILES], tables[0:1, 128:128 + TILES]))
            link(dve.tensor_copy(start[:, :], startf[:, :]))
            link(dve.tensor_tensor(runlen[:, :], runs[:, 1:TILES + 1], startf[:, 0:TILES], ALU.subtract))
            link(dve.tensor_reduce(verdict[0:1, 2:3], runlen[:, :], AX.X, ALU.max))
            link(dve.tensor_scalar(verdict[0:1, 3:4], verdict[0:1, 2:3], float(WIN), None, ALU.is_gt))
            link(dve.tensor_tensor(verdict[0:1, 4:5], tables[0:1, 192:193], verdict[0:1, 3:4], ALU.add))
            link(dve.tensor_scalar(verdict[0:1, 5:6], verdict[0:1, 4:5], 0.5, None, ALU.is_gt))
            dve.tensor_copy(flag[:, :], verdict[0:1, 5:6]).then_inc(s_flag, 1)
            dve.wait_ge(s_small, 48)
            dve.tensor_scalar(onepe[:, 1:2], onepe[:, 0:1], 1.0, None, ALU.add).then_inc(s_const, 1)
            dve.wait_ge(s_const, CONSTS)
            dve.wait_ge(s_flag, 1)

            general = dve.value_load(flag[0:1, 0:1], min_val=0, max_val=1)
            with dve.If(general > 0):
                same = before[0:GT, 3 * D:3 * D + GT]
                copies = before[0:GT, 4 * D:4 * D + GT]
                earlier = before[0:GT, 5 * D:5 * D + GT]
                lower = before[0:GT, 6 * D:6 * D + GT]
                dve.tensor_scalar(lower, iota_row[0:GT, 0:GT], iota_col[0:GT, 0:1], None,
                                  ALU.is_lt).then_inc(g_dve, 1)
                with dve.Fori(0, GTILES) as t:
                    dve.wait_ge(g_edge, 32 * t + 32)
                    dve.wait_ge(g_dve, 7 * t + 1)
                    dve.tensor_copy(boundary[0:GT, 0:1], rowdst[0:GT, 0:1]).then_inc(g_dve, 1)
                    dve.wait_ge(g_dve, 7 * t + 2)
                    dve.tensor_copy(copies, boundary[0:GT, 0:1].to_broadcast([GT, GT])).then_inc(g_dve, 1)
                    dve.wait_ge(g_pe, 2 * t + 1)
                    dve.wait_ge(g_dve, 7 * t + 3)
                    dve.tensor_scalar(same, acc[0][0:GT, 0:GT], boundary[0:GT, 0:1], None,
                                      ALU.is_equal).then_inc(g_dve, 1)
                    dve.wait_ge(g_dve, 7 * t + 4)
                    dve.tensor_tensor(earlier, same, lower, ALU.mult).then_inc(g_dve, 1)
                    dve.wait_ge(g_dve, 7 * t + 5)
                    dve.tensor_reduce(boundary[0:GT, 1:2], earlier, AX.X, ALU.add).then_inc(g_dve, 1)
                    dve.wait_ge(g_dve, 7 * t + 6)
                    dve.scalar_tensor_tensor(out=rowdst[0:GT, 1:2], in0=boundary[0:GT, 1:2], scalar=FAR,
                                             in1=boundary[0:GT, 0:1], op0=ALU.mult,
                                             op1=ALU.add).then_inc(g_dve, 1)
                    dve.wait_ge(g_pe, 2 * t + 2)
                    dve.wait_ge(g_got, 32 * t + 32)
                    dve.wait_ge(g_dve, 7 * t + 7)
                    dve.tensor_tensor(raw[0:GT, 2, :], acc[1][0:GT, :], raw[0:GT, 1, :],
                                      ALU.add).then_inc(g_dve, 1)

            def cut_weights(q):
                dve.wait_ge(s_whi, q + 1)
                if q < TC:
                    to, hi = w1[1][:, q, :], w1[0][:, q, :]
                else:
                    j = 2 * (q - TC)
                    to, hi = (w2[s][:, j:j + 2, :].rearrange("p c n -> p (c n)") for s in (1, 0))
                dve.tensor_tensor(to, wstage[:, q % 2, :], hi.bitcast(F32), ALU.subtract).then_inc(s_wlo, 1)

            def window_f32(T, slot, lap, first=False):
                dve.wait_ge(s_win[slot], 32 * lap + 32)
                if not first:
                    dve.wait_ge(s_winT, T)
                dve.tensor_copy(winf[0:SLOTS, :, :], win[0:SLOTS, slot, :, :]).then_inc(s_winf, 1)

            def window_tables(T, slot):
                dve.wait_ge(s_winT, T + 1)
                dve.tensor_copy(idx[:, slot, :], tables[:, 0:SLOTS]).then_inc(s_idx, 1)
                dve.tensor_scalar(place[:, slot, :], tables[:, SLOTS:2 * SLOTS],
                                  first_node[:, bass.ds(T, 1)], None, ALU.subtract).then_inc(s_place, 1)

            def one_hots(T, i, slot, first=False):
                dve.wait_ge(s_place, T + 1)
                if not first:
                    dve.wait_ge(s_seg, SLOTS * (T - 1))
                dve.tensor_tensor(onehot[:, i, :, :],
                                  iota_row[:, 0:TN].unsqueeze(1).to_broadcast([P, SLOTS, TN]),
                                  place[:, slot, :].unsqueeze(2).to_broadcast([P, SLOTS, TN]),
                                  ALU.is_equal).then_inc(s_onehot, 1)

            def make_rst(T, i, slot, lap, first):
                dve.wait_ge(s_seg, SLOTS * (T + 1))
                dve.wait_ge(s_x[slot], 16 * lap + 16)
                if not first:
                    dve.wait_ge(s_turn, T - 1)
                dve.scalar_tensor_tensor(out=rst[0:TN, i, :], in0=xt[0:TN, slot, :], scalar=onepe[0:TN, 1:2],
                                         in1=acc[i][0:TN, :], op0=ALU.mult, op1=ALU.add).then_inc(s_rst, 1)

            def rst_lo(T, i, half):
                dve.wait_ge(s_rhi, T + 1)
                cols = slice(i * TN, (i + 1) * TN)
                dve.tensor_tensor(rstT[1][:, half, :, cols], turned[:, :, 0:TN],
                                  rstT[0][:, half, :, cols].bitcast(F32), ALU.subtract).then_inc(s_rlo, 1)

            def h_lo(m, jp):
                dve.wait_ge(s_hhi, PAIRS * m + jp + 1)
                dve.tensor_tensor(hT[1][:, 2 * jp:2 * jp + 2, :], hfull[:, jp % 2, :, :],
                                  hT[0][:, 2 * jp:2 * jp + 2, :].bitcast(F32), ALU.subtract).then_inc(s_hlo, 1)

            def residuals(F, f, slot, stores):
                dve.wait_ge(s_y, F + 1)
                if stores is not None:
                    dve.wait_ge(s_store[f], stores)
                dve.scalar_tensor_tensor(out=z[0:TN, f, :], in0=xt[0:TN, slot, :], scalar=2.0,
                                         in1=y[f][0:TN, :], op0=ALU.mult, op1=ALU.add).then_inc(s_z1, 1)
                dve.wait_ge(s_z1, F + 1)
                dve.tensor_tensor(z[0:TN, f, :], z[0:TN, f, :], b2b[0:TN, :], ALU.add).then_inc(s_z2, 1)
                dve.wait_ge(s_z2, F + 1)
                dve.bn_stats(moments[0:TN, f, :], z[0:TN, f, :]).then_inc(s_mom, 1)
                wait_apart(dve, s_mom, F + 1)
                dve.bn_aggr(meanvar[0:TN, f, :], moments[0:TN, f, :]).then_inc(s_mv, 1)

            def normalise(F, f):
                dve.wait_ge(s_std, F + 1)
                dve.reciprocal(rstd[0:TN, f:f + 1], std[0:TN, f:f + 1]).then_inc(s_rstd, 1)
                dve.wait_ge(s_rstd, F + 1)
                dve.tensor_scalar(z[0:TN, f, :], z[0:TN, f, :], meanvar[0:TN, f, 0:1], rstd[0:TN, f:f + 1],
                                  ALU.subtract, ALU.mult).then_inc(s_norm, 1)

            def group(g, res, lap):
                T0 = 2 * g
                static = type(g) is int
                half = 0 if res == 0 else 1
                for p in range(STEPS):
                    i, k = p // SLOTS, p % SLOTS
                    T = T0 + i
                    dve.wait_ge(s_mhi, SLOTS * T + k + 1)
                    at = (res + i + k) % RING
                    dve.tensor_tensor(msg[1][:, at, :], raw[:, k, :], msg[0][:, at, :].bitcast(F32),
                                      ALU.subtract).then_inc(s_mlo, 1)
                    if static and T == 0 and k % 2 == 0 and k // 2 < WPIECES:
                        cut_weights(k // 2)
                    if k == STEP_WINDOW_F32:
                        window_f32(T + 2, (res + i + 2) % 4, lap + (res + i + 2) // 4)
                    if k == STEP_TABLES:
                        window_tables(T + 2, (res + i + 2) % 4)
                    if k == STEP_ONEHOT:
                        one_hots(T + 1, 1 - i, (res + i + 1) % 4, static and T < 1)
                    if k == STEP_RST and not (static and T == 0):
                        make_rst(T - 1, 1 - i, (res + i - 1) % 4, lap + (res + i - 1) // 4, static and T < 3)
                    if k == STEP_RST_LO and not (static and T == 0):
                        rst_lo(T - 1, 1 - i, half if i else 1 - half)
                    for jp in range(PAIRS):
                        if p == HLO_STEP[jp] and not (static and g < 1):
                            h_lo(g - 1, jp)
                        if p == HLO_STEP[jp] - STEPS and not (static and g < 2):
                            h_lo(g - 2, jp)
                    for f in range(2):
                        if p == Z_STEP[f] and not (static and g < 2):
                            residuals(T0 - 4 + f, f, (res + f) % 4,
                                      None if static and g < 3 else 16 * (g - 2))
                        if p == NORM_STEP[f] and not (static and g < 2):
                            normalise(T0 - 4 + f, f)

            for T in range(2):
                window_f32(T, T, 0, T == 0)
                window_tables(T, T)
            one_hots(0, 0, 0, True)
            pair = run_groups(group)
            with dve.Fori(1, GROUPS // 2) as it:
                pair(it)
            last = GROUPS - 1
            h_lo(last - 1, PAIRS - 1)
            make_rst(TILES - 1, 1, (TILES - 1) % 4, (TILES - 1) // 4, False)
            rst_lo(TILES - 1, 1, last % 2)
            for F in range(TILES - 4, TILES):
                if F == TILES - 2:
                    for jp in range(PAIRS):
                        h_lo(last, jp)
                f = F % 2
                residuals(F, f, F % 4, 16 * (F // 2))
                if f == 1:
                    normalise(F - 1, 0)
                    normalise(F, 1)

        @block.tensor
        def _(pe):
            pe.wait_ge(s_prep, PREP_BELOW)
            pe.wait_ge(s_const, CONSTS - 1)
            for b in range(BLK):
                mm = pe.matmul(tables[0:TILES, 0:1], below[0:RP, b, :], ones[0:RP, :],
                               start=(b == 0), stop=(b == BLK - 1))
            mm.then_inc(s_prep_pe, 1)
            pe.wait_ge(s_prep, PREP_BOUNDARY)
            pe.matmul(tables[0:1, 64:64 + TILES], boundary[0:TILES, 2:3], ident[0:TILES, 0:TILES],
                      start=True, stop=True)
            pe.matmul(tables[0:1, 128:128 + TILES], boundary[0:TILES, 3:4], ident[0:TILES, 0:TILES],
                      start=True, stop=True)
            pe.matmul(tables[0:1, 192:193], verdict[0:RP, 1:2], ones[0:RP, :],
                      start=True, stop=True).then_inc(s_prep_pe, 1)

            pe.wait_ge(s_flag, 1)
            general = pe.value_load(flag[0:1, 0:1], min_val=0, max_val=1)
            with pe.If(general > 0):
                same = before[0:GT, 3 * D:3 * D + GT]
                copies = before[0:GT, 4 * D:4 * D + GT]
                with pe.Fori(0, GTILES) as t:
                    pe.wait_ge(g_dve, 7 * t + 3)
                    pe.matmul(acc[0][0:GT, 0:GT], copies, ident[0:GT, 0:GT],
                              start=True, stop=True).then_inc(g_pe, 1)
                    pe.wait_ge(g_dve, 7 * t + 4)
                    pe.wait_ge(g_got, 32 * t + 32)
                    pe.matmul(acc[1][0:GT, :], same, raw[0:GT, 0, :],
                              start=True, stop=True).then_inc(g_pe, 1)

            def window_T(T, first=False):
                if not first:
                    wait_apart(pe, s_place, T)
                wait_apart(pe, s_winf, T + 1)
                for s in range(2):
                    mm = pe.transpose(tables[:, s * SLOTS:(s + 1) * SLOTS], winf[0:SLOTS, s, :],
                                      ident[0:SLOTS, 0:SLOTS])
                mm.then_inc(s_winT, 1)

            def rst_T(T, i, first):
                pe.wait_ge(s_rst, T + 1)
                if not first:
                    pe.wait_ge(s_rlo, T)
                for c in range(TC):
                    mm = pe.transpose(turned[:, c, 0:TN], rst[0:TN, i, c * P:(c + 1) * P],
                                      ident[0:TN, 0:TN])
                mm.then_inc(s_turn, 1)

            def layer1(m, half, first):
                for n in range(HC * TC * 3):
                    j, c, term = n // (TC * 3), n // 3 % TC, n % 3
                    jp, jj = j // 2, j % 2
                    if n == 0:
                        pe.wait_ge(s_rlo, 2 * m + 2)
                        if first:
                            pe.wait_ge(s_wlo, WPIECES)
                    if c == 0 and term == 0 and jj == 0 and not (first and jp < 2):
                        pe.wait_ge(s_relu, HC * m + 2 * jp - 2)
                    a, b = ((0, 0), (0, 1), (1, 0))[term]
                    mm = pe.matmul(hp[jp % 2][:, jj, :], w1[a][:, c, j * P:(j + 1) * P], rstT[b][:, half, c, :],
                                   start=(c == 0 and term == 0), stop=(c == TC - 1 and term == 2))
                    if c == TC - 1 and term == 2:
                        mm.then_inc(s_mm1, 1)
                    yield

            def layer2(m, first):
                for n in range(2 * HC * 3):
                    f, j, term = n // (HC * 3), n // 3 % HC, n % 3
                    if j == 0 and term == 0 and not first:
                        pe.wait_ge(s_z1, 2 * m + f - 1)
                    if f == 0 and j % 2 == 0 and term == 0:
                        pe.wait_ge(s_hlo, PAIRS * m + j // 2 + 1)
                    a, b = ((0, 0), (0, 1), (1, 0))[term]
                    mm = pe.matmul(y[f][0:TN, :], hT[a][:, j, f * TN:(f + 1) * TN], w2[b][:, j, :],
                                   start=(j == 0 and term == 0), stop=(j == HC - 1 and term == 2))
                    if j == HC - 1 and term == 2:
                        mm.then_inc(s_y, 1)
                    yield

            def take(work, n):
                for _ in range(n):
                    next(work, None)

            def group(g, res, lap):
                T0 = 2 * g
                static = type(g) is int
                half = 0 if res == 0 else 1
                one = layer1(g - 1, 1 - half, static and g < 2)
                two = layer2(g - 2, static and g < 3)
                n1, n2 = HC * TC * 3, 2 * HC * 3
                rest = STEPS - OUT_STEPS
                for p in range(STEPS):
                    i, k = p // SLOTS, p % SLOTS
                    T = T0 + i
                    if k == 0:
                        pe.wait_ge(s_onehot, T + 1)
                        if not (static and T < 2):
                            pe.wait_ge(s_rst, T - 1)
                    pe.wait_ge(s_mlo, SLOTS * T + k + 1)
                    at = (res + i + k) % RING
                    for s in range(2):
                        mm = pe.matmul(acc[i][0:TN, :], onehot[:, i, k, :], msg[s][:, at, :],
                                       start=(k == 0 and s == 0), stop=(k == SLOTS - 1 and s == 1))
                    mm.then_inc(s_seg, 1)
                    if k == STEP_WINDOW_T:
                        window_T(T + 2)
                    if k == STEP_RST_T and not (static and T == 0):
                        rst_T(T - 1, 1 - i, static and T == 1)
                    if p < OUT_STEPS:
                        if not (static and g < 2):
                            take(two, n2 * (p + 1) // OUT_STEPS - n2 * p // OUT_STEPS)
                    elif not (static and g < 1):
                        q = p - OUT_STEPS
                        take(one, n1 * (q + 1) // rest - n1 * q // rest)

            for T in range(2):
                window_T(T, T == 0)
            pair = run_groups(group)
            with pe.Fori(1, GROUPS // 2) as it:
                pair(it)
            last = GROUPS - 1
            rst_T(TILES - 1, 1, False)
            take(layer2(last - 1, False), 2 * HC * 3)
            take(layer1(last, last % 2, False), HC * TC * 3)
            take(layer2(last, False), 2 * HC * 3)


PREP_BELOW = 1 + BLK
PREP_ROWIDX = PREP_BELOW + 2
PREP_BOUNDARY = PREP_ROWIDX + 3 + 4
CONSTS = 7

_INS = ['x', 'src', 'dst', 'L0_gnn_W1', 'L0_gnn_b1', 'L0_gnn_W2', 'L0_gnn_b2', 'L0_gnn_eps']


def kernel(**inputs):
    import numpy as _np
    import concourse.bacc as _bacc
    from concourse.bass_utils import run_bass_kernel_spmd as _run

    nc = _bacc.Bacc("TRN2", target_bir_lowering=False, num_devices=1)
    arrays, args = {}, []
    for name in _INS:
        a = _np.ascontiguousarray(inputs[name])
        arrays[f"in_{name}_dram"] = a
        args.append(nc.dram_tensor(f"in_{name}_dram", a.shape, mybir.dt.from_np(a.dtype), kind="ExternalInput").ap())
    args.append(nc.dram_tensor("out_dram", (N, D), F32, kind="ExternalOutput").ap())
    build(nc, *args)
    r = _run(nc, [arrays], core_ids=[0])
    return r.results[0]["out_dram"]
```

```python
from contextlib import ExitStack

import concourse.bass as bass
from concourse import mybir

F32 = mybir.dt.float32
F32R = mybir.dt.float32r
I32 = mybir.dt.int32
ALU = mybir.AluOpType
ACT = mybir.ActivationFunctionType
AX = mybir.AxisListType

P = 128
N = 6250
E = 100000
D = 512
HID = 1024
TN = 125
TILES = N // TN
GROUPS = TILES // 2
SLOTS = 17
WIN = SLOTS * P
PAIRED = (SLOTS + 1) // 2
STEPS = 2 * PAIRED
RING = 3
AHEAD = 3
TC = D // P
HC = HID // P
PAIRS = HC // 2
ROW = 160
RP = 125
BLK = E // (ROW * RP)
GT = 125
GTILES = E // GT
WPIECES = 8
LN_EPS = 1e-5
FAR = 1.0e6
assert TN * TILES == N and ROW * RP * BLK == E and GT * GTILES == E

AT_WINDOW_F32 = 0
AT_WINDOW_T = 1
AT_TABLES = 5
AT_RST = 2
AT_RST_T = 3
AT_RST_HI = 6
AT_RST_LO = 7
AT_ONEHOT = (3, 4, 6)
OUT_STEPS = 8
RELU_STEP = (13, 15, 17, 19)
HLO_STEP = (14, 16, 18, 20)
Z_STEP = (6, 10)
B2_STEP = (7, 11)
MOM_STEP = (8, 12)
SQRT_STEP = (10, 14)
RSTD_STEP = (11, 15)
NORM_STEP = (13, 17)
ONEHOT_PIECES = ((0, 6), (6, 12), (12, SLOTS))


def build(nc, x, src, dst, W1, b1, W2, b2, eps, out):
    neigh = nc.dram_tensor("neigh", (N, D), F32, kind="Internal").ap()
    one_src = nc.dram_tensor("one_src", (TILES + AHEAD, WIN), I32, kind="Internal").ap()
    one_dst = nc.dram_tensor("one_dst", (TILES + AHEAD, WIN), I32, kind="Internal").ap()

    with ExitStack() as ctx:
        def sb(name, shape, dt):
            return ctx.enter_context(nc.sbuf_tensor(name, shape, dt))

        def pb(name, shape):
            return ctx.enter_context(nc.psum_tensor(name, shape, F32))

        def sem(name):
            return ctx.enter_context(nc.semaphore(name))

        w1 = [sb(f"w1_{s}", [P, TC, HID], F32R) for s in ("hi", "lo")]
        w2 = [sb(f"w2_{s}", [P, HC, D], F32R) for s in ("hi", "lo")]
        raw = sb("raw", [P, SLOTS, D], F32)
        msg = [sb(f"msg_{s}", [P, RING, 2, D], F32R) for s in ("hi", "lo")]
        onehot = sb("onehot", [P, 2, SLOTS, TN], F32R)
        xt = sb("xt", [P, 4, D], F32)
        rst = sb("rst", [P, 2, D], F32)
        rstT = [sb(f"rstT_{s}", [P, 2, TC, 2 * TN], F32R) for s in ("hi", "lo")]
        late = sb("late", [P, 2, HID], F32)
        hT = [sb(f"hT_{s}", [P, HC, 2 * TN], F32R) for s in ("hi", "lo")]
        wstage = late
        z = late[:, 0, :].rearrange("p (f d) -> p f d", f=2)
        hfull = late[:, 1, 0:8 * TN].rearrange("p (a b n) -> p a b n", a=2, b=2)
        b2b = sb("b2b", [P, D], F32)
        b1c = sb("b1c", [P, HC], F32)
        onepe = sb("onepe", [P, 2], F32)
        epsln = sb("epsln", [P, 1], F32)
        ident = sb("ident", [P, P], F32)
        iota_row = sb("iota_row", [P, P], F32)
        iota_col = sb("iota_col", [P, 1], F32)
        first_node = sb("first_node", [P, TILES + AHEAD], F32)
        first_node_col = sb("first_node_col", [P, 1], F32)
        ones = sb("ones", [P, 1], F32)
        win = sb("win", [P, 4, 2, P], I32)
        winf = sb("winf", [P, 2, P], F32)
        idx = sb("idx", [P, 4, SLOTS], I32)
        place = sb("place", [P, 4, SLOTS], F32)
        moments = sb("moments", [P, 2, 6], F32)
        meanvar = sb("meanvar", [P, 2, 2], F32)
        std = sb("std", [P, 2], F32)
        rstd = sb("rstd", [P, 2], F32)
        shift = sb("shift", [P, 2], F32)
        below = sb("below", [P, BLK, TILES], F32)
        lastf = sb("lastf", [P, BLK], F32)
        boundary = sb("boundary", [P, 4], F32)
        rowidx = sb("rowidx", [P, 1], I32)
        rowdst = sb("rowdst", [P, ROW], I32)
        rowcmp = sb("rowcmp", [P, ROW], F32)
        runs = sb("runs", [1, TILES + 1], F32)
        startf = sb("startf", [1, TILES + AHEAD], F32)
        start = sb("start", [1, TILES + AHEAD], I32)
        runlen = sb("runlen", [1, TILES], F32)
        verdict = sb("verdict", [P, 8], F32)
        flag = sb("flag", [1, 1], I32)
        before = raw[:, :, :].rearrange("p s d -> p (s d)")
        dsti = before[0:RP, 0:BLK * (ROW + 1)].bitcast(I32).rearrange("p (b j) -> p b j", b=BLK)
        falls = before[0:RP, 1024:1024 + BLK * ROW].rearrange("p (b j) -> p b j", b=BLK)

        node = before[0:TILES, 4 * D:4 * D + WIN].bitcast(I32)
        zeros = before[:, 9 * D:9 * D + WIN]
        same, copies, earlier, lower = (before[0:GT, 15 * D + i * P:15 * D + i * P + GT] for i in range(4))

        acc = [pb(f"acc{i}", [P, D]) for i in range(2)]
        tables = pb("tables", [P, D])
        turned = pb("turned", [P, TC, P])
        hp = [pb(f"hp{i}", [P, 2, 2 * TN]) for i in range(2)]
        y = [pb(f"y{i}", [P, D]) for i in range(2)]

        s_iota = sem("s_iota")
        s_const = sem("s_const")
        s_small = sem("s_small")
        s_dst = sem("s_dst")
        s_prep = sem("s_prep")
        s_prep_pe = sem("s_prep_pe")
        s_rowdst = sem("s_rowdst")
        s_flag = sem("s_flag")
        s_wload = [sem(f"s_wload{i}") for i in range(2)]
        s_whi = sem("s_whi")
        s_wlo = sem("s_wlo")
        s_win = [sem(f"s_win{i}") for i in range(4)]
        s_winf = sem("s_winf")
        s_winT = sem("s_winT")
        s_idx = sem("s_idx")
        s_place = sem("s_place")
        s_onehot = sem("s_onehot")
        s_gather = [sem(f"s_gather{k}") for k in range(PAIRED)]
        s_mhi = sem("s_mhi")
        s_mlo = sem("s_mlo")
        s_seg = sem("s_seg")
        s_x = [sem(f"s_x{i}") for i in range(4)]
        s_rst = sem("s_rst")
        s_turn = sem("s_turn")
        s_rhi = sem("s_rhi")
        s_rlo = sem("s_rlo")
        s_mm1 = sem("s_mm1")
        s_relu = sem("s_relu")
        s_hhi = sem("s_hhi")
        s_hlo = sem("s_hlo")
        s_y = sem("s_y")
        s_z1 = sem("s_z1")
        s_z2 = sem("s_z2")
        s_mom = sem("s_mom")
        s_mv = sem("s_mv")
        s_std = sem("s_std")
        s_rstd = sem("s_rstd")
        s_shift = sem("s_shift")
        s_norm = sem("s_norm")
        s_store = [sem(f"s_store{i}") for i in range(2)]
        g_dve = sem("g_dve")
        g_pool = sem("g_pool")
        g_zero = sem("g_zero")
        g_table = sem("g_table")
        g_edge = sem("g_edge")
        g_got = sem("g_got")
        g_pe = sem("g_pe")
        g_put = sem("g_put")
        g_step = sem("g_step")

        block = ctx.enter_context(nc.Block())

        def wait_apart(eng, signal, value):
            value = value if type(value) is int else eng.to_reg(value)
            eng.wait_ge(s_flag, 1)
            eng.wait_ge(signal, value)

        def run_groups(group):
            for g in range(3):
                group(g, 2 * g % 4, 2 * g // 4)

            def pair(it):
                group(2 * it + 1, 2, it)
                group(2 * it + 2, 0, it + 1)
            return pair

        @block.sync
        def _(sp):
            rows = dst.rearrange("(b q j) -> q b j", b=BLK, q=RP)
            sp.dma_start(dsti[:, :, 0:ROW], rows).then_inc(s_dst, 16)
            nxt = dst.rearrange("(r j) -> r j", j=ROW)
            with nc.allow_non_contiguous_dma(reason="one element of each row of dst"):
                for b in range(BLK):
                    n = RP if b < BLK - 1 else RP - 1
                    sp.dma_start(dsti[0:n, b, ROW:ROW + 1],
                                 nxt[b * RP + 1:b * RP + 1 + n, 0:1]).then_inc(s_dst, 16)
                sp.dma_start(dsti[RP - 1:RP, BLK - 1, ROW:ROW + 1],
                             nxt[BLK * RP - 1:BLK * RP, ROW - 1:ROW]).then_inc(s_dst, 16)
            sp.dma_start(onepe[:, 0:1], eps.partition_broadcast(P)).then_inc(s_small, 16)
            sp.dma_start(b2b[:, :], b2.partition_broadcast(P)).then_inc(s_small, 16)
            with nc.allow_non_contiguous_dma(reason="the bias of the hidden layer, one a partition"):
                sp.dma_start(b1c[:, :], b1.rearrange("(c p) -> p c", p=P)).then_inc(s_small, 16)

            def load_x(t, slot):
                sp.dma_start(xt[0:TN, slot, :], x[bass.ds(t * TN, TN), :]).then_inc(s_x[slot], 16)

            def load_weights(q):
                if q >= 2:
                    sp.wait_ge(s_wlo, q - 1)
                if q < TC:
                    piece = W1[q * P:(q + 1) * P, :]
                    sp.dma_start(wstage[:, q % 2, :], piece).then_inc(s_wload[q % 2], 16)
                else:
                    j = 2 * (q - TC)
                    piece = W2[j * P:(j + 2) * P, :].rearrange("(c p) n -> p c n", p=P)
                    room = wstage[:, q % 2, :].rearrange("p (c n) -> p c n", c=2)
                    sp.dma_start(room, piece).then_inc(s_wload[q % 2], 16)

            for q in range(2):
                load_weights(q)
            for t in range(4):
                load_x(t, t)

            def main(window_of):
                def load_window(t, slot):
                    s_rows, d_rows = window_of(t)
                    sp.dma_start(win[0:SLOTS, slot, 0, :], s_rows).then_inc(s_win[slot], 16)
                    sp.dma_start(win[0:SLOTS, slot, 1, :], d_rows).then_inc(s_win[slot], 16)

                for t in range(AHEAD):
                    load_window(t, t)
                for q in range(2, WPIECES):
                    load_weights(q)

                def group(g, res, lap):
                    T0 = 2 * g
                    for i in range(2):
                        T = T0 + i
                        slot = (res + i + 3) % 4
                        if not (type(T) is int and T == 0):
                            sp.wait_ge(s_winf, T)
                        load_window(T + 3, slot)
                        if i == 0 and not (type(g) is int and g < 2):
                            for F, f in ((T0 - 4, 0), (T0 - 3, 1)):
                                sp.wait_ge(s_z1, F + 1)
                                load_x(F + 4, (res + f) % 4)
                                sp.wait_ge(s_norm, F + 1)
                                store(F, f)

                def store(F, f):
                    sp.dma_start(out[bass.ds(F * TN, TN), :], z[0:TN, f, :]).then_inc(s_store[f], 16)

                pair = run_groups(group)
                with sp.Fori(1, GROUPS // 2) as it:
                    pair(it)
                for F in range(TILES - 4, TILES):
                    sp.wait_ge(s_norm, F + 1)
                    store(F, F % 2)
                for f in range(2):
                    sp.wait_ge(s_store[f], 16 * TILES // 2)
                for slot in range(4):
                    n = len(range(slot, TILES + AHEAD, 4))
                    sp.wait_ge(s_win[slot], 32 * n)

            def window_of_edges(t):
                at = sp.value_load(start[0:1, bass.ds(t, 1)], min_val=0, max_val=E - WIN)
                return tuple(a[bass.ds(at, WIN)].rearrange("(k p) -> k p", p=P) for a in (src, dst))

            def window_of_nodes(t):
                return tuple(a[bass.ds(t, 1), :].rearrange("a (k p) -> (a k) p", p=P)
                             for a in (one_src, one_dst))

            sp.wait_ge(s_flag, 1)
            general = sp.value_load(flag[0:1, 0:1], min_val=0, max_val=1)
            with sp.If(general > 0):
                with nc.allow_non_contiguous_dma(reason="an edge a partition"):
                    with sp.Fori(0, GTILES) as t:
                        sp.wait_ge(g_step, t + 1)
                        sp.dma_start(rowidx[0:GT, :], src[bass.ds(t * GT, GT)].rearrange("(p a) -> p a", a=1)
                                     ).then_inc(g_edge, 16)
                        sp.dma_start(rowdst[0:GT, 0:1], dst[bass.ds(t * GT, GT)].rearrange("(p a) -> p a", a=1)
                                     ).then_inc(g_edge, 16)
                sp.wait_ge(g_table, 32)
                main(window_of_nodes)
            with sp.Else():
                main(window_of_edges)

        @block.gpsimd
        def _(pool):
            pool.iota(iota_row[:, :], [[1, P]], base=0, channel_multiplier=0,
                      allow_small_or_imprecise_dtypes=True).then_inc(s_iota, 1)
            pool.iota(iota_col[:, :], [[0, 1]], base=0, channel_multiplier=1,
                      allow_small_or_imprecise_dtypes=True).then_inc(s_iota, 1)
            pool.iota(first_node[:, :], [[TN, TILES + AHEAD]], base=0, channel_multiplier=0,
                      allow_small_or_imprecise_dtypes=True).then_inc(s_iota, 1)
            pool.iota(first_node_col[:, :], [[0, 1]], base=0, channel_multiplier=TN,
                      allow_small_or_imprecise_dtypes=True).then_inc(s_iota, 1)
            pool.wait_ge(s_prep, PREP_ROWIDX)
            pool.indirect_dma_start(
                out=rowdst[0:TILES, :], out_offset=None, in_=dst.rearrange("(r j) -> r j", j=ROW),
                in_offset=bass.IndirectOffsetOnAxis(ap=rowidx[0:TILES, 0:1], axis=0)).then_inc(s_rowdst, 16)

            def main(table):
                def group(g, res, lap):
                    T0 = 2 * g
                    for i in range(2):
                        T = T0 + i
                        wait_apart(pool, s_idx, T + 1)
                        for k in range(SLOTS):
                            if k % 2 == 0 and not (type(T) is int and T == 0):
                                wait_apart(pool, s_mlo, PAIRED * (T - 1) + k // 2 + 1)
                            pool.indirect_dma_start(
                                out=raw[:, k, :], out_offset=None, in_=table[:, :],
                                in_offset=bass.IndirectOffsetOnAxis(
                                    ap=idx[:, (res + i) % 4, k:k + 1], axis=0)).then_inc(s_gather[k // 2], 16)

                pair = run_groups(group)
                with pool.Fori(1, GROUPS // 2) as it:
                    pair(it)

            pool.wait_ge(s_flag, 1)
            general = pool.value_load(flag[0:1, 0:1], min_val=0, max_val=1)
            with pool.If(general > 0):
                pool.memset(node, 0).then_inc(g_pool, 1)
                pool.wait_ge(g_pool, 1)
                pool.iota(node[:, 0:TN], [[1, TN]], base=0, channel_multiplier=TN).then_inc(g_pool, 1)
                pool.wait_ge(g_pool, 2)
                pool.dma_start(one_src[0:TILES, :], node).then_inc(g_table, 16)
                pool.wait_ge(g_table, 16)
                pool.memset(node[:, TN:WIN], -1000000).then_inc(g_pool, 1)
                pool.wait_ge(g_pool, 3)
                pool.dma_start(one_dst[0:TILES, :], node).then_inc(g_table, 16)
                pool.memset(zeros, 0.0).then_inc(g_pool, 1)
                pool.wait_ge(g_pool, 4)
                pool.wait_ge(g_table, 32)
                for t in (one_src, one_dst):
                    pool.dma_start(t[TILES:TILES + AHEAD, :],
                                   zeros[0:AHEAD, :].bitcast(I32)).then_inc(g_zero, 16)
                with pool.Fori(0, TILES) as t:
                    pool.dma_start(neigh[bass.ds(t * TN, TN), :], zeros[0:TN, 0:D]).then_inc(g_zero, 16)
                pool.wait_ge(g_zero, 16 * (TILES + 2))
                pool.memset(before[0:1, 0:1], 0.0).then_inc(g_step, 1)
                with pool.Fori(0, GTILES) as t:
                    wait_apart(pool, g_edge, 32 * t + 32)
                    pool.indirect_dma_start(
                        out=raw[0:GT, 0, :], out_offset=None, in_=x[:, :],
                        in_offset=bass.IndirectOffsetOnAxis(ap=rowidx[0:GT, 0:1], axis=0)).then_inc(g_got, 16)
                    pool.indirect_dma_start(
                        out=raw[0:GT, 1, :], out_offset=None, in_=neigh[:, :],
                        in_offset=bass.IndirectOffsetOnAxis(ap=rowdst[0:GT, 0:1], axis=0)).then_inc(g_got, 16)
                    wait_apart(pool, g_dve, 7 * t + 8)
                    pool.indirect_dma_start(
                        out=neigh[:, :], out_offset=bass.IndirectOffsetOnAxis(ap=rowdst[0:GT, 1:2], axis=0),
                        in_=raw[0:GT, 2, :], in_offset=None, bounds_check=N - 1,
                        oob_is_err=False).then_inc(g_put, 16)
                    wait_apart(pool, g_put, 16 * t + 16)
                    pool.memset(before[0:1, 0:1], 0.0).then_inc(g_step, 1)
                pool.wait_ge(g_step, GTILES + 1)
                main(neigh)
            with pool.Else():
                main(x)

        @block.scalar
        def _(act):
            def cut_weights(q):
                act.wait_ge(s_wload[q % 2], 16 * (q // 2 + 1))
                to = w1[0][:, q, :] if q < TC else \
                    w2[0][:, 2 * (q - TC):2 * (q - TC) + 2, :].rearrange("p c n -> p (c n)")
                act.activation(to, wstage[:, q % 2, :], ACT.Copy).then_inc(s_whi, 1)

            def rst_hi(T, i, half, m_seen, first):
                act.wait_ge(s_turn, T + 1)
                if not first:
                    act.wait_ge(s_mm1, HC * m_seen)
                act.activation(rstT[0][:, half, :, i * TN:(i + 1) * TN], turned[:, :, 0:TN],
                               ACT.Copy).then_inc(s_rhi, 1)

            def relu_pair(m, jp, first):
                act.wait_ge(s_mm1, HC * m + 2 * jp + 2)
                for jj in range(2):
                    j = 2 * jp + jj
                    if not (first and jp < 2):
                        act.wait_ge(s_hlo, PAIRS * m + jp - 1)
                    act.activation(hfull[:, jp % 2, jj, :], hp[jp % 2][:, jj, :], ACT.Relu,
                                   bias=b1c[:, j:j + 1]).then_inc(s_relu, 1)
                act.wait_ge(s_relu, HC * m + 2 * jp + 2)
                if not first:
                    act.wait_ge(s_y, 2 * m)
                act.activation(hT[0][:, 2 * jp:2 * jp + 2, :], hfull[:, jp % 2, :, :],
                               ACT.Copy).then_inc(s_hhi, 1)

            def root(F, f):
                act.wait_ge(s_mv, F + 1)
                act.activation(std[0:TN, f:f + 1], meanvar[0:TN, f, 1:2], ACT.Sqrt,
                               bias=epsln[0:TN, 0:1]).then_inc(s_std, 1)

            def normalise(F, f):
                act.wait_ge(s_shift, F + 1)
                act.activation(z[0:TN, f, :], z[0:TN, f, :], ACT.Identity, bias=shift[0:TN, f:f + 1],
                               scale=rstd[0:TN, f:f + 1]).then_inc(s_norm, 1)

            def window_f32(T, slot, lap, first=False):
                act.wait_ge(s_win[slot], 32 * lap + 32)
                if not first:
                    act.wait_ge(s_winT, T)
                act.activation(winf[0:SLOTS, :, :], win[0:SLOTS, slot, :, :], ACT.Copy).then_inc(s_winf, 1)

            def group(g, res, lap):
                T0 = 2 * g
                static = type(g) is int
                half = 0 if res == 0 else 1
                for p in range(STEPS):
                    i, kp = p // PAIRED, p % PAIRED
                    T = T0 + i
                    n = min(2, SLOTS - 2 * kp)
                    act.wait_ge(s_gather[kp], 16 * n * (T + 1))
                    if not (static and T == 0 and kp < RING):
                        act.wait_ge(s_seg, PAIRED * T + kp + 1 - RING)
                    act.activation(msg[0][:, p % RING, 0:n, :], raw[:, 2 * kp:2 * kp + n, :],
                                   ACT.Copy).then_inc(s_mhi, 1)
                    if static and T == 0 and kp < WPIECES:
                        cut_weights(kp)
                    if kp == AT_WINDOW_F32:
                        window_f32(T + 2, (res + i + 2) % 4, lap + (res + i + 2) // 4)
                    if kp == AT_RST_HI and not (static and T == 0):
                        if i == 0:
                            rst_hi(T - 1, 1, 1 - half, g - 2, static and g < 3)
                        else:
                            rst_hi(T - 1, 0, half, g - 1, static and g < 2)
                    for jp in range(PAIRS):
                        if p == RELU_STEP[jp] and not (static and g < 1):
                            relu_pair(g - 1, jp, static and g == 1)
                        if p == RELU_STEP[jp] - STEPS and not (static and g < 2):
                            relu_pair(g - 2, jp, static and g == 2)
                    for f in range(2):
                        if p == SQRT_STEP[f] and not (static and g < 2):
                            root(T0 - 4 + f, f)
                        if p == NORM_STEP[f] and not (static and g < 2):
                            normalise(T0 - 4 + f, f)

            act.wait_ge(s_small, 48)
            act.wait_ge(s_const, CONSTS)
            for T in range(2):
                window_f32(T, T, 0, T == 0)
            pair = run_groups(group)
            with act.Fori(1, GROUPS // 2) as it:
                pair(it)
            last = GROUPS - 1
            for jp in range(PAIRS):
                if RELU_STEP[jp] >= STEPS:
                    relu_pair(last - 1, jp, False)
            rst_hi(TILES - 1, 1, last % 2, last - 1, False)
            for f in range(2):
                root(TILES - 4 + f, f)
                normalise(TILES - 4 + f, f)
            for jp in range(PAIRS):
                relu_pair(last, jp, False)
            for f in range(2):
                root(TILES - 2 + f, f)
                normalise(TILES - 2 + f, f)

        @block.vector
        def _(dve):
            count = [0]

            def link(ins):
                count[0] += 1
                ins.then_inc(s_prep, 1)
                dve.wait_ge(s_prep, count[0])

            dve.memset(ones[:, :], 1.0).then_inc(s_const, 1)
            dve.memset(epsln[:, :], LN_EPS).then_inc(s_const, 1)
            dve.memset(startf[:, :], 0.0).then_inc(s_const, 1)
            dve.memset(runs[:, :], float(E)).then_inc(s_const, 1)
            dve.memset(verdict[:, :], 0.0).then_inc(s_const, 1)
            dve.wait_ge(s_iota, 4)
            dve.tensor_scalar(ident[:, :], iota_row[:, :], iota_col[:, 0:1], None,
                              ALU.is_equal).then_inc(s_const, 1)
            dve.wait_ge(s_dst, 16 * (BLK + 2))
            link(dve.tensor_copy(lastf[0:RP, :], dsti[:, :, ROW - 1]))
            for b in range(BLK):
                link(dve.tensor_scalar(below[0:RP, b, :], first_node[0:RP, 0:TILES], lastf[0:RP, b:b + 1],
                                       None, ALU.is_gt))
            assert count[0] == PREP_BELOW
            dve.wait_ge(s_prep_pe, 1)
            link(dve.tensor_scalar(boundary[0:TILES, 0:1], tables[0:TILES, 0:1], float(BLK * RP - 1), None,
                                   ALU.min))
            link(dve.tensor_copy(rowidx[0:TILES, :], boundary[0:TILES, 0:1]))
            assert count[0] == PREP_ROWIDX
            link(dve.tensor_tensor(falls, dsti[:, :, 0:ROW], dsti[:, :, 1:ROW + 1], ALU.subtract))
            link(dve.tensor_reduce(verdict[0:RP, 0:1], before[0:RP, 1024:1024 + BLK * ROW], AX.X, ALU.max))
            link(dve.tensor_scalar(verdict[0:RP, 1:2], verdict[0:RP, 0:1], 0.0, None, ALU.is_gt))
            dve.wait_ge(s_rowdst, 16)
            link(dve.tensor_scalar(rowcmp[0:TILES, :], rowdst[0:TILES, :], first_node_col[0:TILES, 0:1], None,
                                   ALU.is_lt))
            link(dve.tensor_reduce(boundary[0:TILES, 1:2], rowcmp[0:TILES, :], AX.X, ALU.add))
            link(dve.scalar_tensor_tensor(out=boundary[0:TILES, 2:3], in0=boundary[0:TILES, 0:1],
                                          scalar=float(ROW), in1=boundary[0:TILES, 1:2],
                                          op0=ALU.mult, op1=ALU.add))
            link(dve.tensor_scalar(boundary[0:TILES, 3:4], boundary[0:TILES, 2:3], float(E - WIN), None,
                                   ALU.min))
            assert count[0] == PREP_BOUNDARY
            dve.wait_ge(s_prep_pe, 2)
            link(dve.tensor_copy(runs[0:1, 0:TILES], tables[0:1, 64:64 + TILES]))
            link(dve.tensor_copy(startf[0:1, 0:TILES], tables[0:1, 128:128 + TILES]))
            link(dve.tensor_copy(start[:, :], startf[:, :]))
            link(dve.tensor_tensor(runlen[:, :], runs[:, 1:TILES + 1], startf[:, 0:TILES], ALU.subtract))
            link(dve.tensor_reduce(verdict[0:1, 2:3], runlen[:, :], AX.X, ALU.max))
            link(dve.tensor_scalar(verdict[0:1, 3:4], verdict[0:1, 2:3], float(WIN), None, ALU.is_gt))
            link(dve.tensor_tensor(verdict[0:1, 4:5], tables[0:1, 192:193], verdict[0:1, 3:4], ALU.add))
            link(dve.tensor_scalar(verdict[0:1, 5:6], verdict[0:1, 4:5], 0.5, None, ALU.is_gt))
            dve.tensor_copy(flag[:, :], verdict[0:1, 5:6]).then_inc(s_flag, 1)
            dve.wait_ge(s_small, 48)
            dve.tensor_scalar(onepe[:, 1:2], onepe[:, 0:1], 1.0, None, ALU.add).then_inc(s_const, 1)
            dve.wait_ge(s_const, CONSTS)
            dve.wait_ge(s_flag, 1)

            general = dve.value_load(flag[0:1, 0:1], min_val=0, max_val=1)
            with dve.If(general > 0):
                dve.tensor_scalar(lower, iota_row[0:GT, 0:GT], iota_col[0:GT, 0:1], None,
                                  ALU.is_lt).then_inc(g_dve, 1)
                with dve.Fori(0, GTILES) as t:
                    dve.wait_ge(g_edge, 32 * t + 32)
                    dve.wait_ge(g_dve, 7 * t + 1)
                    dve.tensor_copy(boundary[0:GT, 0:1], rowdst[0:GT, 0:1]).then_inc(g_dve, 1)
                    dve.wait_ge(g_dve, 7 * t + 2)
                    dve.tensor_copy(copies, boundary[0:GT, 0:1].to_broadcast([GT, GT])).then_inc(g_dve, 1)
                    dve.wait_ge(g_pe, 2 * t + 1)
                    dve.wait_ge(g_dve, 7 * t + 3)
                    dve.tensor_scalar(same, acc[0][0:GT, 0:GT], boundary[0:GT, 0:1], None,
                                      ALU.is_equal).then_inc(g_dve, 1)
                    dve.wait_ge(g_dve, 7 * t + 4)
                    dve.tensor_tensor(earlier, same, lower, ALU.mult).then_inc(g_dve, 1)
                    dve.wait_ge(g_dve, 7 * t + 5)
                    dve.tensor_reduce(boundary[0:GT, 1:2], earlier, AX.X, ALU.add).then_inc(g_dve, 1)
                    dve.wait_ge(g_dve, 7 * t + 6)
                    dve.scalar_tensor_tensor(out=rowdst[0:GT, 1:2], in0=boundary[0:GT, 1:2], scalar=FAR,
                                             in1=boundary[0:GT, 0:1], op0=ALU.mult,
                                             op1=ALU.add).then_inc(g_dve, 1)
                    dve.wait_ge(g_pe, 2 * t + 2)
                    dve.wait_ge(g_got, 32 * t + 32)
                    dve.wait_ge(g_dve, 7 * t + 7)
                    dve.tensor_tensor(raw[0:GT, 2, :], acc[1][0:GT, :], raw[0:GT, 1, :],
                                      ALU.add).then_inc(g_dve, 1)

            def cut_weights(q):
                dve.wait_ge(s_whi, q + 1)
                if q < TC:
                    to, hi = w1[1][:, q, :], w1[0][:, q, :]
                else:
                    j = 2 * (q - TC)
                    to, hi = (w2[s][:, j:j + 2, :].rearrange("p c n -> p (c n)") for s in (1, 0))
                dve.tensor_tensor(to, wstage[:, q % 2, :], hi.bitcast(F32), ALU.subtract).then_inc(s_wlo, 1)

            def window_tables(T, slot):
                dve.wait_ge(s_winT, T + 1)
                dve.tensor_copy(idx[:, slot, :], tables[:, 0:SLOTS]).then_inc(s_idx, 1)
                dve.tensor_scalar(place[:, slot, :], tables[:, SLOTS:2 * SLOTS],
                                  first_node[:, bass.ds(T, 1)], None, ALU.subtract).then_inc(s_place, 1)

            def one_hots(T, i, slot, piece, first=False):
                dve.wait_ge(s_place, T + 1)
                if not first:
                    dve.wait_ge(s_seg, PAIRED * (T - 1))
                k0, k1 = ONEHOT_PIECES[piece]
                shape = [P, k1 - k0, TN]
                dve.tensor_tensor(onehot[:, i, k0:k1, :],
                                  iota_row[:, 0:TN].unsqueeze(1).to_broadcast(shape),
                                  place[:, slot, k0:k1].unsqueeze(2).to_broadcast(shape),
                                  ALU.is_equal).then_inc(s_onehot, 1)

            def make_rst(T, i, slot, lap, first):
                dve.wait_ge(s_seg, PAIRED * (T + 1))
                dve.wait_ge(s_x[slot], 16 * lap + 16)
                if not first:
                    dve.wait_ge(s_turn, T - 1)
                dve.scalar_tensor_tensor(out=rst[0:TN, i, :], in0=xt[0:TN, slot, :], scalar=onepe[0:TN, 1:2],
                                         in1=acc[i][0:TN, :], op0=ALU.mult, op1=ALU.add).then_inc(s_rst, 1)

            def rst_lo(T, i, half):
                dve.wait_ge(s_rhi, T + 1)
                cols = slice(i * TN, (i + 1) * TN)
                dve.tensor_tensor(rstT[1][:, half, :, cols], turned[:, :, 0:TN],
                                  rstT[0][:, half, :, cols].bitcast(F32), ALU.subtract).then_inc(s_rlo, 1)

            def h_lo(m, jp):
                dve.wait_ge(s_hhi, PAIRS * m + jp + 1)
                dve.tensor_tensor(hT[1][:, 2 * jp:2 * jp + 2, :], hfull[:, jp % 2, :, :],
                                  hT[0][:, 2 * jp:2 * jp + 2, :].bitcast(F32), ALU.subtract).then_inc(s_hlo, 1)

            def residuals(F, f, slot, stores):
                dve.wait_ge(s_y, F + 1)
                if stores is not None:
                    dve.wait_ge(s_store[f], stores)
                dve.scalar_tensor_tensor(out=z[0:TN, f, :], in0=xt[0:TN, slot, :], scalar=2.0,
                                         in1=y[f][0:TN, :], op0=ALU.mult, op1=ALU.add).then_inc(s_z1, 1)

            def add_b2(F, f):
                dve.wait_ge(s_z1, F + 1)
                dve.tensor_tensor(z[0:TN, f, :], z[0:TN, f, :], b2b[0:TN, :], ALU.add).then_inc(s_z2, 1)

            def take_moments(F, f):
                dve.wait_ge(s_z2, F + 1)
                dve.bn_stats(moments[0:TN, f, :], z[0:TN, f, :]).then_inc(s_mom, 1)
                wait_apart(dve, s_mom, F + 1)
                dve.bn_aggr(meanvar[0:TN, f, :], moments[0:TN, f, :]).then_inc(s_mv, 1)

            def scale_shift(F, f):
                dve.wait_ge(s_std, F + 1)
                dve.reciprocal(rstd[0:TN, f:f + 1], std[0:TN, f:f + 1]).then_inc(s_rstd, 1)
                dve.wait_ge(s_rstd, F + 1)
                dve.scalar_tensor_tensor(out=shift[0:TN, f:f + 1], in0=meanvar[0:TN, f, 0:1], scalar=-1.0,
                                         in1=rstd[0:TN, f:f + 1], op0=ALU.mult,
                                         op1=ALU.mult).then_inc(s_shift, 1)

            def group(g, res, lap):
                T0 = 2 * g
                static = type(g) is int
                half = 0 if res == 0 else 1
                for p in range(STEPS):
                    i, kp = p // PAIRED, p % PAIRED
                    T = T0 + i
                    n = min(2, SLOTS - 2 * kp)
                    dve.wait_ge(s_mhi, PAIRED * T + kp + 1)
                    dve.tensor_tensor(msg[1][:, p % RING, 0:n, :], raw[:, 2 * kp:2 * kp + n, :],
                                      msg[0][:, p % RING, 0:n, :].bitcast(F32), ALU.subtract).then_inc(s_mlo, 1)
                    if static and T == 0 and kp < WPIECES:
                        cut_weights(kp)
                    if kp == AT_TABLES:
                        window_tables(T + 2, (res + i + 2) % 4)
                    for piece in range(3):
                        if kp == AT_ONEHOT[piece]:
                            one_hots(T + 1, 1 - i, (res + i + 1) % 4, piece, static and T < 1)
                    if kp == AT_RST and not (static and T == 0):
                        make_rst(T - 1, 1 - i, (res + i - 1) % 4, lap + (res + i - 1) // 4, static and T < 3)
                    if kp == AT_RST_LO and not (static and T == 0):
                        rst_lo(T - 1, 1 - i, half if i else 1 - half)
                    for jp in range(PAIRS):
                        if p == HLO_STEP[jp] and not (static and g < 1):
                            h_lo(g - 1, jp)
                        if p == HLO_STEP[jp] - STEPS and not (static and g < 2):
                            h_lo(g - 2, jp)
                    if static and g < 2:
                        continue
                    for f in range(2):
                        F = T0 - 4 + f
                        if p == Z_STEP[f]:
                            residuals(F, f, (res + f) % 4, None if static and g < 3 else 16 * (g - 2))
                        if p == B2_STEP[f]:
                            add_b2(F, f)
                        if p == MOM_STEP[f]:
                            take_moments(F, f)
                        if p == RSTD_STEP[f]:
                            scale_shift(F, f)

            for T in range(2):
                window_tables(T, T)
            for piece in range(3):
                one_hots(0, 0, 0, piece, True)
            pair = run_groups(group)
            with dve.Fori(1, GROUPS // 2) as it:
                pair(it)
            last = GROUPS - 1
            for jp in range(PAIRS):
                if HLO_STEP[jp] >= STEPS:
                    h_lo(last - 1, jp)
            make_rst(TILES - 1, 1, (TILES - 1) % 4, (TILES - 1) // 4, False)
            rst_lo(TILES - 1, 1, last % 2)
            for F in range(TILES - 4, TILES):
                if F == TILES - 2:
                    for jp in range(PAIRS):
                        h_lo(last, jp)
                residuals(F, F % 2, F % 4, 16 * (F // 2))
                add_b2(F, F % 2)
                take_moments(F, F % 2)
                scale_shift(F, F % 2)

        @block.tensor
        def _(pe):
            pe.wait_ge(s_prep, PREP_BELOW)
            pe.wait_ge(s_const, CONSTS - 1)
            for b in range(BLK):
                mm = pe.matmul(tables[0:TILES, 0:1], below[0:RP, b, :], ones[0:RP, :],
                               start=(b == 0), stop=(b == BLK - 1))
            mm.then_inc(s_prep_pe, 1)
            pe.wait_ge(s_prep, PREP_BOUNDARY)
            pe.matmul(tables[0:1, 64:64 + TILES], boundary[0:TILES, 2:3], ident[0:TILES, 0:TILES],
                      start=True, stop=True)
            pe.matmul(tables[0:1, 128:128 + TILES], boundary[0:TILES, 3:4], ident[0:TILES, 0:TILES],
                      start=True, stop=True)
            pe.matmul(tables[0:1, 192:193], verdict[0:RP, 1:2], ones[0:RP, :],
                      start=True, stop=True).then_inc(s_prep_pe, 1)

            pe.wait_ge(s_flag, 1)
            general = pe.value_load(flag[0:1, 0:1], min_val=0, max_val=1)
            with pe.If(general > 0):
                with pe.Fori(0, GTILES) as t:
                    pe.wait_ge(g_dve, 7 * t + 3)
                    pe.matmul(acc[0][0:GT, 0:GT], copies, ident[0:GT, 0:GT],
                              start=True, stop=True).then_inc(g_pe, 1)
                    pe.wait_ge(g_dve, 7 * t + 4)
                    pe.wait_ge(g_got, 32 * t + 32)
                    pe.matmul(acc[1][0:GT, :], same, raw[0:GT, 0, :],
                              start=True, stop=True).then_inc(g_pe, 1)

            def window_T(T, first=False):
                if not first:
                    wait_apart(pe, s_place, T)
                wait_apart(pe, s_winf, T + 1)
                for s in range(2):
                    mm = pe.transpose(tables[:, s * SLOTS:(s + 1) * SLOTS], winf[0:SLOTS, s, :],
                                      ident[0:SLOTS, 0:SLOTS])
                mm.then_inc(s_winT, 1)

            def rst_T(T, i, first):
                pe.wait_ge(s_rst, T + 1)
                if not first:
                    pe.wait_ge(s_rlo, T)
                for c in range(TC):
                    mm = pe.transpose(turned[:, c, 0:TN], rst[0:TN, i, c * P:(c + 1) * P],
                                      ident[0:TN, 0:TN])
                mm.then_inc(s_turn, 1)

            def layer1(m, half, first):
                for n in range(HC * TC * 3):
                    j, c, term = n // (TC * 3), n // 3 % TC, n % 3
                    jp, jj = j // 2, j % 2
                    if n == 0:
                        pe.wait_ge(s_rlo, 2 * m + 2)
                        if first:
                            pe.wait_ge(s_wlo, WPIECES)
                    if c == 0 and term == 0 and jj == 0 and not (first and jp < 2):
                        pe.wait_ge(s_relu, HC * m + 2 * jp - 2)
                    a, b = ((0, 0), (0, 1), (1, 0))[term]
                    mm = pe.matmul(hp[jp % 2][:, jj, :], w1[a][:, c, j * P:(j + 1) * P], rstT[b][:, half, c, :],
                                   start=(c == 0 and term == 0), stop=(c == TC - 1 and term == 2))
                    if c == TC - 1 and term == 2:
                        mm.then_inc(s_mm1, 1)
                    yield

            def layer2(m, first):
                for n in range(2 * HC * 3):
                    f, j, term = n // (HC * 3), n // 3 % HC, n % 3
                    if j == 0 and term == 0 and not first:
                        pe.wait_ge(s_z1, 2 * m + f - 1)
                    if f == 0 and j % 2 == 0 and term == 0:
                        pe.wait_ge(s_hlo, PAIRS * m + j // 2 + 1)
                    a, b = ((0, 0), (0, 1), (1, 0))[term]
                    mm = pe.matmul(y[f][0:TN, :], hT[a][:, j, f * TN:(f + 1) * TN], w2[b][:, j, :],
                                   start=(j == 0 and term == 0), stop=(j == HC - 1 and term == 2))
                    if j == HC - 1 and term == 2:
                        mm.then_inc(s_y, 1)
                    yield

            def take(work, n):
                for _ in range(n):
                    next(work, None)

            def group(g, res, lap):
                T0 = 2 * g
                static = type(g) is int
                half = 0 if res == 0 else 1
                one = layer1(g - 1, 1 - half, static and g < 2)
                two = layer2(g - 2, static and g < 3)
                n1, n2 = HC * TC * 3, 2 * HC * 3
                rest = STEPS - OUT_STEPS
                for p in range(STEPS):
                    i, kp = p // PAIRED, p % PAIRED
                    T = T0 + i
                    for piece in range(3):
                        if 2 * kp == ONEHOT_PIECES[piece][0]:
                            pe.wait_ge(s_onehot, 3 * T + piece + 1)
                    if kp == 0 and not (static and T < 2):
                        pe.wait_ge(s_rst, T - 1)
                    pe.wait_ge(s_mlo, PAIRED * T + kp + 1)
                    for k in range(2 * kp, min(2 * kp + 2, SLOTS)):
                        for s in range(2):
                            mm = pe.matmul(acc[i][0:TN, :], onehot[:, i, k, :], msg[s][:, p % RING, k % 2, :],
                                           start=(k == 0 and s == 0), stop=(k == SLOTS - 1 and s == 1))
                    mm.then_inc(s_seg, 1)
                    if kp == AT_WINDOW_T:
                        window_T(T + 2)
                    if kp == AT_RST_T and not (static and T == 0):
                        rst_T(T - 1, 1 - i, static and T == 1)
                    if p < OUT_STEPS:
                        if not (static and g < 2):
                            take(two, n2 * (p + 1) // OUT_STEPS - n2 * p // OUT_STEPS)
                    elif not (static and g < 1):
                        q = p - OUT_STEPS
                        take(one, n1 * (q + 1) // rest - n1 * q // rest)

            for T in range(2):
                window_T(T, T == 0)
            pair = run_groups(group)
            with pe.Fori(1, GROUPS // 2) as it:
                pair(it)
            last = GROUPS - 1
            rst_T(TILES - 1, 1, False)
            take(layer2(last - 1, False), 2 * HC * 3)
            take(layer1(last, last % 2, False), HC * TC * 3)
            take(layer2(last, False), 2 * HC * 3)


PREP_BELOW = 1 + BLK
PREP_ROWIDX = PREP_BELOW + 2
PREP_BOUNDARY = PREP_ROWIDX + 3 + 4
CONSTS = 7

_INS = ['x', 'src', 'dst', 'L0_gnn_W1', 'L0_gnn_b1', 'L0_gnn_W2', 'L0_gnn_b2', 'L0_gnn_eps']


def kernel(**inputs):
    import numpy as _np
    import concourse.bacc as _bacc
    from concourse.bass_utils import run_bass_kernel_spmd as _run

    nc = _bacc.Bacc("TRN2", target_bir_lowering=False, num_devices=1)
    arrays, args = {}, []
    for name in _INS:
        a = _np.ascontiguousarray(inputs[name])
        arrays[f"in_{name}_dram"] = a
        args.append(nc.dram_tensor(f"in_{name}_dram", a.shape, mybir.dt.from_np(a.dtype), kind="ExternalInput").ap())
    args.append(nc.dram_tensor("out_dram", (N, D), F32, kind="ExternalOutput").ap())
    build(nc, *args)
    r = _run(nc, [arrays], core_ids=[0])
    return r.results[0]["out_dram"]
```

```python
from contextlib import ExitStack

import concourse.bass as bass
from concourse import mybir

F32 = mybir.dt.float32
F32R = mybir.dt.float32r
I32 = mybir.dt.int32
ALU = mybir.AluOpType
ACT = mybir.ActivationFunctionType
AX = mybir.AxisListType

P = 128
N = 6250
E = 100000
D = 512
HID = 1024
TN = 125
TILES = N // TN
GROUPS = TILES // 2
SLOTS = 17
WIN = SLOTS * P
PAIRED = (SLOTS + 1) // 2
STEPS = 2 * PAIRED
WHOLE = 4
RING = 3
AHEAD = 3
TC = D // P
HC = HID // P
PAIRS = HC // 2
L1_PRODUCTS = HC * TC * 3
L2_PRODUCTS = 2 * HC * 3
ROW = 160
RP = 125
BLK = E // (ROW * RP)
GT = 125
GTILES = E // GT
WPIECES = 8
ROOM = (0, 1, 2, 0, 1, 0, 1, 0)
LN_EPS = 1e-5
FAR = 1.0e6
assert TN * TILES == N and ROW * RP * BLK == E and GT * GTILES == E

AT_WINDOW_F32 = 0
AT_WINDOW_T = 1
AT_TABLES = 5
AT_RST = 2
AT_RST_T = 2
AT_RST_HI = 5
AT_RST_LO = 5
AT_ONEHOT = (3, 4, 6)
FIRST_WINDOW_F32 = (0, 3)
FIRST_WINDOW_T = (0, 4)
FIRST_TABLES = (1, 5)
FIRST_ONEHOT = (1, 2, 3)
ACT_CUT_STEP = (2, 10, 14, 17, 20)
CUT_STEP = (0, 3, 10, 14, 17, 20)
BESIDE = ((5, "w", 4), (6, "x", 0), (10, "w", 5), (12, "x", 1), (13, "w", 6), (16, "w", 7),
          (18, "x", 2), (20, "x", 3))
L1_STEP, L1_STEPS = 5, 9
L2_STEP, L2_STEPS = 14, 9
RELU_STEP = (10, 12, 15, 17)
HLO_STEP = (10, 14, 16, 18)
DOUBLE_STEP = (7, 8)
Z_STEP = (8, 9)
MOM_STEP = (8, 10)
SQRT_STEP = (10, 12)
RSTD_STEP = (11, 13)
NORM_STEP = (12, 15)
ONEHOT_PIECES = ((0, 6), (6, 12), (12, SLOTS))


def build(nc, x, src, dst, W1, b1, W2, b2, eps, out):
    neigh = nc.dram_tensor("neigh", (N, D), F32, kind="Internal").ap()
    one_src = nc.dram_tensor("one_src", (TILES + AHEAD, WIN), I32, kind="Internal").ap()
    one_dst = nc.dram_tensor("one_dst", (TILES + AHEAD, WIN), I32, kind="Internal").ap()

    with ExitStack() as ctx:
        def sb(name, shape, dt):
            return ctx.enter_context(nc.sbuf_tensor(name, shape, dt))

        def pb(name, shape):
            return ctx.enter_context(nc.psum_tensor(name, shape, F32))

        def sem(name):
            return ctx.enter_context(nc.semaphore(name))

        w1 = [sb(f"w1_{s}", [P, TC, HID], F32R) for s in ("hi", "lo")]
        w2 = [sb(f"w2_{s}", [P, HC, D], F32R) for s in ("hi", "lo")]
        raw = sb("raw", [P, SLOTS, D], F32)
        msg = [sb(f"msg_{s}", [P, RING, 2, D], F32R) for s in ("hi", "lo")]
        onehot = sb("onehot", [P, 2, SLOTS, TN], F32R)
        xt = sb("xt", [P, 4, D], F32)
        rst = sb("rst", [P, 2, D], F32)
        rstT = [sb(f"rstT_{s}", [P, 2, TC, 2 * TN], F32R) for s in ("hi", "lo")]
        late = sb("late", [P, 2, HID], F32)
        hT = [sb(f"hT_{s}", [P, HC, 2 * TN], F32R) for s in ("hi", "lo")]
        z = late[:, 0, :].rearrange("p (f d) -> p f d", f=2)
        hfull = late[:, 1, 0:8 * TN].rearrange("p (a b n) -> p a b n", a=2, b=2)
        b2b = sb("b2b", [P, D], F32)
        b1c = sb("b1c", [P, HC], F32)
        onepe = sb("onepe", [P, 2], F32)
        epsln = sb("epsln", [P, 1], F32)
        ident = sb("ident", [P, P], F32)
        iota_row = sb("iota_row", [P, P], F32)
        iota_col = sb("iota_col", [P, 1], F32)
        first_node = sb("first_node", [P, TILES + AHEAD], F32)
        first_node_col = sb("first_node_col", [P, 1], F32)
        ones = sb("ones", [P, 1], F32)
        win = sb("win", [P, 4, 2, P], I32)
        winf = sb("winf", [P, 2, P], F32)
        idx = sb("idx", [P, 4, SLOTS], I32)
        place = sb("place", [P, 4, SLOTS], F32)
        moments = sb("moments", [P, 2, 6], F32)
        meanvar = sb("meanvar", [P, 2, 2], F32)
        std = sb("std", [P, 2], F32)
        rstd = sb("rstd", [P, 2], F32)
        shift = sb("shift", [P, 2], F32)
        below = sb("below", [P, BLK, TILES], F32)
        lastf = sb("lastf", [P, BLK], F32)
        boundary = sb("boundary", [P, 4], F32)
        rowidx = sb("rowidx", [P, 1], I32)
        rowdst = sb("rowdst", [P, ROW], I32)
        rowcmp = sb("rowcmp", [P, ROW], F32)
        runs = sb("runs", [1, TILES + 1], F32)
        startf = sb("startf", [1, TILES], F32)
        start = sb("start", [1, TILES + AHEAD], I32)
        runlen = sb("runlen", [1, TILES], F32)
        verdict = sb("verdict", [P, 8], F32)
        flag = sb("flag", [1, 1], I32)
        rooms = (late[:, 0, :], late[:, 1, :], rst[:, :, :].rearrange("p i d -> p (i d)"))
        wstage = [rooms[ROOM[q]] for q in range(WPIECES)]
        xroom = xt[0:RP, :, :].rearrange("p s d -> p (s d)")
        dsti = xroom[:, 0:BLK * (ROW + 1)].bitcast(I32).rearrange("p (b j) -> p b j", b=BLK)
        falls = xroom[:, 2 * D:2 * D + BLK * ROW]

        before = raw[:, :, :].rearrange("p s d -> p (s d)")
        node = before[0:TILES, 4 * D:4 * D + WIN].bitcast(I32)
        zeros = before[:, 9 * D:9 * D + WIN]
        same, copies, earlier, lower = (before[0:GT, 15 * D + i * P:15 * D + i * P + GT] for i in range(4))

        acc = [pb(f"acc{i}", [P, D]) for i in range(2)]
        tables = pb("tables", [P, D])
        turned = pb("turned", [P, TC, P])
        hp = [pb(f"hp{i}", [P, 2, 2 * TN]) for i in range(2)]
        y = [pb(f"y{i}", [P, D]) for i in range(2)]

        s_iota = sem("s_iota")
        s_const = sem("s_const")
        s_small = sem("s_small")
        s_b2 = sem("s_b2")
        s_dst = sem("s_dst")
        s_next = sem("s_next")
        s_prep = sem("s_prep")
        s_prep_pe = sem("s_prep_pe")
        s_rowdst = sem("s_rowdst")
        s_start0 = sem("s_start0")
        s_start = sem("s_start")
        s_flag = sem("s_flag")
        s_wload = [sem(f"s_wload{q}") for q in range(WPIECES)]
        s_whi = sem("s_whi")
        s_wlo = sem("s_wlo")
        s_win = [sem(f"s_win{i}") for i in range(4)]
        s_winf = sem("s_winf")
        s_go = sem("s_go")
        s_winT = sem("s_winT")
        s_idx = sem("s_idx")
        s_place = sem("s_place")
        s_onehot = sem("s_onehot")
        s_gather = [sem(f"s_gather{k}") for k in range(PAIRED)]
        s_mhi = sem("s_mhi")
        s_mlo = sem("s_mlo")
        s_seg = sem("s_seg")
        s_x = [sem(f"s_x{i}") for i in range(4)]
        s_rst = sem("s_rst")
        s_turn = sem("s_turn")
        s_rhi = sem("s_rhi")
        s_rlo = sem("s_rlo")
        s_mm1 = sem("s_mm1")
        s_relu = sem("s_relu")
        s_hhi = sem("s_hhi")
        s_hlo = sem("s_hlo")
        s_y = sem("s_y")
        s_double = sem("s_double")
        s_z = sem("s_z")
        s_mom = sem("s_mom")
        s_mv = sem("s_mv")
        s_std = sem("s_std")
        s_rstd = sem("s_rstd")
        s_shift = sem("s_shift")
        s_norm = sem("s_norm")
        s_store = [sem(f"s_store{i}") for i in range(2)]
        g_dve = sem("g_dve")
        g_pool = sem("g_pool")
        g_zero = sem("g_zero")
        g_table = sem("g_table")
        g_edge = sem("g_edge")
        g_got = sem("g_got")
        g_pe = sem("g_pe")
        g_put = sem("g_put")
        g_step = sem("g_step")
        g_win = sem("g_win")
        g_winf = sem("g_winf")
        g_winT = sem("g_winT")
        g_tab = sem("g_tab")
        g_onehot = sem("g_onehot")
        g_again = sem("g_again")

        block = ctx.enter_context(nc.Block())

        def wait_apart(eng, signal, value):
            value = value if type(value) is int else eng.to_reg(value)
            eng.wait_ge(s_flag, 1)
            eng.wait_ge(signal, value)

        def weights(q):
            if q < TC:
                return [w[:, q, :] for w in w1]
            j = 2 * (q - TC)
            return [w[:, j:j + 2, :].rearrange("p c n -> p (c n)") for w in w2]

        def left_before(q):
            return max(i for i in range(q) if ROOM[i] == ROOM[q]) + 1

        def run_groups(group):
            for g in range(3):
                group(g, 2 * g % 4, 2 * g // 4)

            def pair(it):
                group(2 * it + 1, 2, it)
                group(2 * it + 2, 0, it + 1)
            return pair

        @block.sync
        def _(sp):
            for s, edges in enumerate((src, dst)):
                sp.dma_start(win[0:SLOTS, 0, s, :],
                             edges[0:WIN].rearrange("(k p) -> k p", p=P)).then_inc(s_win[0], 16)
            rows = dst.rearrange("(b q j) -> q b j", b=BLK, q=RP)
            sp.dma_start(dsti[:, :, 0:ROW], rows).then_inc(s_dst, 16)
            sp.dma_start(onepe[:, 0:1], eps.partition_broadcast(P)).then_inc(s_small, 16)
            with nc.allow_non_contiguous_dma(reason="the bias of the hidden layer, one a partition"):
                sp.dma_start(b1c[:, :], b1.rearrange("(c p) -> p c", p=P)).then_inc(s_small, 16)
            nxt = dst.rearrange("(r j) -> r j", j=ROW)
            with nc.allow_non_contiguous_dma(reason="one element of each row of dst"):
                for b in range(BLK):
                    n = RP if b < BLK - 1 else RP - 1
                    sp.dma_start(dsti[0:n, b, ROW:ROW + 1],
                                 nxt[b * RP + 1:b * RP + 1 + n, 0:1]).then_inc(s_next, 16)
                sp.dma_start(dsti[RP - 1:RP, BLK - 1, ROW:ROW + 1],
                             nxt[BLK * RP - 1:BLK * RP, ROW - 1:ROW]).then_inc(s_next, 16)

            def load_weights(q):
                if q < TC:
                    sp.dma_start(wstage[q], W1[q * P:(q + 1) * P, :]).then_inc(s_wload[q], 16)
                else:
                    j = 2 * (q - TC)
                    sp.dma_start(wstage[q].rearrange("p (c n) -> p c n", c=2),
                                 W2[j * P:(j + 2) * P, :].rearrange("(c p) n -> p c n", p=P)
                                 ).then_inc(s_wload[q], 16)

            for q in range(2):
                load_weights(q)
            sp.wait_ge(s_rowdst, 16)
            load_weights(2)

            def in_two(move, tile_rows, room, signal):
                for r0, r1 in ((0, 112), (112, TN)):
                    move(tile_rows, room, r0, r1, signal)

            def load_rows(t, room, r0, r1, signal):
                sp.dma_start(room[r0:r1, :], x[bass.ds(t * TN + r0, r1 - r0), :]).then_inc(signal, 16)

            def store_rows(t, room, r0, r1, signal):
                sp.dma_start(out[bass.ds(t * TN + r0, r1 - r0), :], room[r0:r1, :]).then_inc(signal, 16)

            def load_x(t, slot):
                in_two(load_rows, t, xt[:, slot, :], s_x[slot])

            def main(window_of):
                def load_window(t, slot):
                    s_rows, d_rows = window_of(t)
                    sp.dma_start(win[0:SLOTS, slot, 0, :], s_rows).then_inc(s_win[slot], 16)
                    sp.dma_start(win[0:SLOTS, slot, 1, :], d_rows).then_inc(s_win[slot], 16)

                def load_rest():
                    for steps, load, which in BESIDE:
                        sp.wait_ge(s_seg, steps)
                        if load == "x":
                            load_x(which, which)
                        else:
                            sp.wait_ge(s_wlo, left_before(which))
                            load_weights(which)
                    sp.dma_start(b2b[:, :], b2.partition_broadcast(P)).then_inc(s_b2, 16)

                load_window(1, 1)
                sp.wait_ge(s_wlo, left_before(3))
                load_weights(3)
                load_window(2, 2)
                def group(g, res, lap):
                    T0 = 2 * g
                    for i in range(2):
                        if not (type(g) is int and g == 0 and i == 0):
                            sp.wait_ge(s_winf, T0 + i)
                        if type(g) is int and g == 0 and i == 1:
                            sp.wait_ge(s_go, 1)
                        load_window(T0 + i + 3, (res + i + 3) % 4)
                    if type(g) is int and g == 0:
                        load_rest()
                    if type(g) is int and g < 2:
                        return
                    for f in range(2):
                        F = T0 - 4 + f
                        sp.wait_ge(s_z, F + 1)
                        load_x(F + 4, (res + f) % 4)
                        sp.wait_ge(s_norm, F + 1)
                        store(F, f)

                def store(F, f):
                    in_two(store_rows, F, z[:, f, :], s_store[f])

                pair = run_groups(group)
                with sp.Fori(1, GROUPS // 2) as it:
                    pair(it)
                for F in range(TILES - 4, TILES):
                    sp.wait_ge(s_norm, F + 1)
                    store(F, F % 2)
                for f in range(2):
                    sp.wait_ge(s_store[f], 32 * TILES // 2)
                for slot in range(4):
                    n = len(range(slot, TILES + AHEAD, 4))
                    sp.wait_ge(s_win[slot], 32 * n)

            def window_of_edges(t):
                at = sp.value_load(start[0:1, bass.ds(t, 1)], min_val=0, max_val=E - WIN)
                return tuple(a[bass.ds(at, WIN)].rearrange("(k p) -> k p", p=P) for a in (src, dst))

            def window_of_nodes(t):
                return tuple(a[bass.ds(t, 1), :].rearrange("a (k p) -> (a k) p", p=P)
                             for a in (one_src, one_dst))

            sp.wait_ge(s_flag, 1)
            general = sp.value_load(flag[0:1, 0:1], min_val=0, max_val=1)
            with sp.If(general > 0):
                with nc.allow_non_contiguous_dma(reason="an edge a partition"):
                    with sp.Fori(0, GTILES) as t:
                        sp.wait_ge(g_step, t + 1)
                        sp.dma_start(rowidx[0:GT, :], src[bass.ds(t * GT, GT)].rearrange("(p a) -> p a", a=1)
                                     ).then_inc(g_edge, 16)
                        sp.dma_start(rowdst[0:GT, 0:1], dst[bass.ds(t * GT, GT)].rearrange("(p a) -> p a", a=1)
                                     ).then_inc(g_edge, 16)
                sp.wait_ge(g_table, 32)
                for s, edges in enumerate(window_of_nodes(0)):
                    sp.dma_start(win[0:SLOTS, 0, s, :], edges).then_inc(g_win, 16)
                main(window_of_nodes)
            with sp.Else():
                main(window_of_edges)

        @block.gpsimd
        def _(pool):
            pool.iota(iota_row[:, :], [[1, P]], base=0, channel_multiplier=0,
                      allow_small_or_imprecise_dtypes=True).then_inc(s_iota, 1)
            pool.iota(iota_col[:, :], [[0, 1]], base=0, channel_multiplier=1,
                      allow_small_or_imprecise_dtypes=True).then_inc(s_iota, 1)
            pool.iota(first_node[:, :], [[TN, TILES + AHEAD]], base=0, channel_multiplier=0,
                      allow_small_or_imprecise_dtypes=True).then_inc(s_iota, 1)
            pool.iota(first_node_col[:, :], [[0, 1]], base=0, channel_multiplier=TN,
                      allow_small_or_imprecise_dtypes=True).then_inc(s_iota, 1)

            def gather(table, k, slot, signal):
                pool.indirect_dma_start(
                    out=raw[:, k, :], out_offset=None, in_=table[:, :],
                    in_offset=bass.IndirectOffsetOnAxis(ap=idx[:, slot, k:k + 1], axis=0)).then_inc(signal, 16)

            pool.wait_ge(s_idx, 1)
            for k in range(SLOTS):
                if k == 2:
                    pool.wait_ge(s_prep, PREP_ROWIDX)
                    pool.indirect_dma_start(
                        out=rowdst[0:TILES, :], out_offset=None, in_=dst.rearrange("(r j) -> r j", j=ROW),
                        in_offset=bass.IndirectOffsetOnAxis(ap=rowidx[0:TILES, 0:1], axis=0)
                        ).then_inc(s_rowdst, 16)
                gather(x, k, 0, s_gather[k // 2])

            def main(table):
                def group(g, res, lap):
                    T0 = 2 * g
                    for i in range(2):
                        T = T0 + i
                        if type(T) is int and T == 0:
                            continue
                        wait_apart(pool, s_idx, T + 1)
                        for k in range(SLOTS):
                            if k % 2 == 0:
                                if type(T) is int and T == 1 and k // 2 < WHOLE:
                                    pool.wait_ge(s_seg, k // 2 + 1)
                                else:
                                    wait_apart(pool, s_mlo, PAIRED * (T - 1) + k // 2 + 1 - WHOLE)
                            gather(table, k, (res + i) % 4, s_gather[k // 2])

                pair = run_groups(group)
                with pool.Fori(1, GROUPS // 2) as it:
                    pair(it)

            pool.wait_ge(s_flag, 1)
            general = pool.value_load(flag[0:1, 0:1], min_val=0, max_val=1)
            with pool.If(general > 0):
                for k in range(PAIRED):
                    pool.wait_ge(s_gather[k], 16 * min(2, SLOTS - 2 * k))
                pool.memset(node, 0).then_inc(g_pool, 1)
                pool.wait_ge(g_pool, 1)
                pool.iota(node[:, 0:TN], [[1, TN]], base=0, channel_multiplier=TN).then_inc(g_pool, 1)
                pool.wait_ge(g_pool, 2)
                pool.dma_start(one_src[0:TILES, :], node).then_inc(g_table, 16)
                pool.wait_ge(g_table, 16)
                pool.memset(node[:, TN:WIN], -1000000).then_inc(g_pool, 1)
                pool.wait_ge(g_pool, 3)
                pool.dma_start(one_dst[0:TILES, :], node).then_inc(g_table, 16)
                pool.memset(zeros, 0.0).then_inc(g_pool, 1)
                pool.wait_ge(g_pool, 4)
                pool.wait_ge(g_table, 32)
                for t in (one_src, one_dst):
                    pool.dma_start(t[TILES:TILES + AHEAD, :],
                                   zeros[0:AHEAD, :].bitcast(I32)).then_inc(g_zero, 16)
                with pool.Fori(0, TILES) as t:
                    pool.dma_start(neigh[bass.ds(t * TN, TN), :], zeros[0:TN, 0:D]).then_inc(g_zero, 16)
                pool.wait_ge(g_zero, 16 * (TILES + 2))
                pool.memset(before[0:1, 0:1], 0.0).then_inc(g_step, 1)
                with pool.Fori(0, GTILES) as t:
                    wait_apart(pool, g_edge, 32 * t + 32)
                    pool.indirect_dma_start(
                        out=raw[0:GT, 0, :], out_offset=None, in_=x[:, :],
                        in_offset=bass.IndirectOffsetOnAxis(ap=rowidx[0:GT, 0:1], axis=0)).then_inc(g_got, 16)
                    pool.indirect_dma_start(
                        out=raw[0:GT, 1, :], out_offset=None, in_=neigh[:, :],
                        in_offset=bass.IndirectOffsetOnAxis(ap=rowdst[0:GT, 0:1], axis=0)).then_inc(g_got, 16)
                    wait_apart(pool, g_dve, 7 * t + 8)
                    pool.indirect_dma_start(
                        out=neigh[:, :], out_offset=bass.IndirectOffsetOnAxis(ap=rowdst[0:GT, 1:2], axis=0),
                        in_=raw[0:GT, 2, :], in_offset=None, bounds_check=N - 1,
                        oob_is_err=False).then_inc(g_put, 16)
                    wait_apart(pool, g_put, 16 * t + 16)
                    pool.memset(before[0:1, 0:1], 0.0).then_inc(g_step, 1)
                pool.wait_ge(g_step, GTILES + 1)
                pool.wait_ge(g_tab, 2)
                for k in range(SLOTS):
                    gather(neigh, k, 0, g_again)
                main(neigh)
            with pool.Else():
                main(x)

        @block.scalar
        def _(act):
            def cut_weights(q):
                act.wait_ge(s_wload[q], 16)
                act.activation(weights(q)[0], wstage[q], ACT.Copy).then_inc(s_whi, 1)

            def rst_hi(T, i, half, m_seen, first):
                act.wait_ge(s_turn, T + 1)
                if not first:
                    act.wait_ge(s_mm1, HC * m_seen)
                act.activation(rstT[0][:, half, :, i * TN:(i + 1) * TN], turned[:, :, 0:TN],
                               ACT.Copy).then_inc(s_rhi, 1)

            def relu_pair(m, jp, first):
                act.wait_ge(s_mm1, HC * m + 2 * jp + 2)
                for jj in range(2):
                    j = 2 * jp + jj
                    if first and j == 0:
                        act.wait_ge(s_wlo, WPIECES)
                    if not (first and jp < 2):
                        act.wait_ge(s_hlo, PAIRS * m + jp - 1)
                    act.activation(hfull[:, jp % 2, jj, :], hp[jp % 2][:, jj, :], ACT.Relu,
                                   bias=b1c[:, j:j + 1]).then_inc(s_relu, 1)
                act.wait_ge(s_relu, HC * m + 2 * jp + 2)
                if not first:
                    act.wait_ge(s_y, 2 * m)
                act.activation(hT[0][:, 2 * jp:2 * jp + 2, :], hfull[:, jp % 2, :, :],
                               ACT.Copy).then_inc(s_hhi, 1)

            def root(F, f):
                act.wait_ge(s_mv, F + 1)
                act.activation(std[0:TN, f:f + 1], meanvar[0:TN, f, 1:2], ACT.Sqrt,
                               bias=epsln[0:TN, 0:1]).then_inc(s_std, 1)

            def normalise(F, f):
                act.wait_ge(s_shift, F + 1)
                act.activation(z[0:TN, f, :], z[0:TN, f, :], ACT.Identity, bias=shift[0:TN, f:f + 1],
                               scale=rstd[0:TN, f:f + 1]).then_inc(s_norm, 1)

            def window_f32(T, slot, lap, first=False):
                act.wait_ge(s_win[slot], 32 * lap + 32)
                if not first:
                    act.wait_ge(s_winT, T)
                act.activation(winf[0:SLOTS, :, :], win[0:SLOTS, slot, :, :], ACT.Copy).then_inc(s_winf, 1)

            def group(g, res, lap):
                T0 = 2 * g
                static = type(g) is int
                half = 0 if res == 0 else 1
                for p in range(STEPS):
                    i, kp = p // PAIRED, p % PAIRED
                    T = T0 + i
                    n = min(2, SLOTS - 2 * kp)
                    if not (static and T == 0 and kp < WHOLE):
                        act.wait_ge(s_gather[kp], 16 * n * (T + 1))
                        if not (static and p < WHOLE + RING and g == 0):
                            act.wait_ge(s_seg, PAIRED * T + kp + 1 - RING)
                        act.activation(msg[0][:, p % RING, 0:n, :], raw[:, 2 * kp:2 * kp + n, :],
                                       ACT.Copy).then_inc(s_mhi, 1)
                    if static and p + STEPS * g in ACT_CUT_STEP:
                        cut_weights(3 + ACT_CUT_STEP.index(p + STEPS * g))
                    if static and T == 0:
                        for w in range(2):
                            if kp == FIRST_WINDOW_F32[w]:
                                window_f32(1 + w, 1 + w, 0)
                    elif kp == AT_WINDOW_F32:
                        window_f32(T + 2, (res + i + 2) % 4, lap + (res + i + 2) // 4)
                    if kp == AT_RST_HI and not (static and T == 0):
                        if i == 0:
                            rst_hi(T - 1, 1, 1 - half, g - 2, static and g < 3)
                        else:
                            rst_hi(T - 1, 0, half, g - 1, static and g < 2)
                    for jp in range(PAIRS):
                        if p == RELU_STEP[jp] and not (static and g < 1):
                            relu_pair(g - 1, jp, static and g == 1)
                        if p == RELU_STEP[jp] - STEPS and not (static and g < 2):
                            relu_pair(g - 2, jp, static and g == 2)
                    for f in range(2):
                        if p == SQRT_STEP[f] and not (static and g < 2):
                            root(T0 - 4 + f, f)
                        if p == NORM_STEP[f] and not (static and g < 2):
                            normalise(T0 - 4 + f, f)

            window_f32(0, 0, 0, True)
            for q in range(3):
                cut_weights(q)
            act.wait_ge(s_small, 32)
            act.wait_ge(s_const, CONSTS)
            act.wait_ge(s_go, 1)
            pair = run_groups(group)
            with act.Fori(1, GROUPS // 2) as it:
                pair(it)
            last = GROUPS - 1
            for jp in range(PAIRS):
                if RELU_STEP[jp] >= STEPS:
                    relu_pair(last - 1, jp, False)
            rst_hi(TILES - 1, 1, last % 2, last - 1, False)
            for f in range(2):
                root(TILES - 4 + f, f)
                normalise(TILES - 4 + f, f)
            for jp in range(PAIRS):
                relu_pair(last, jp, False)
            for f in range(2):
                root(TILES - 2 + f, f)
                normalise(TILES - 2 + f, f)

        @block.vector
        def _(dve):
            count = [0]

            def link(ins):
                count[0] += 1
                ins.then_inc(s_prep, 1)
                dve.wait_ge(s_prep, count[0])

            dve.memset(ones[:, :], 1.0).then_inc(s_const, 1)
            dve.memset(epsln[:, :], LN_EPS).then_inc(s_const, 1)
            dve.memset(start[:, :], 0).then_inc(s_start0, 1)
            dve.memset(runs[:, :], float(E)).then_inc(s_const, 1)
            dve.memset(verdict[:, :], 0.0).then_inc(s_const, 1)
            dve.wait_ge(s_start0, 1)
            dve.wait_ge(s_iota, 4)
            dve.tensor_scalar(ident[:, :], iota_row[:, :], iota_col[:, 0:1], None,
                              ALU.is_equal).then_inc(s_const, 1)
            def cut_weights(q):
                dve.wait_ge(s_whi, q + 1)
                hi, lo = weights(q)
                dve.tensor_tensor(lo, wstage[q], hi.bitcast(F32), ALU.subtract).then_inc(s_wlo, 1)

            def window_tables(T, slot):
                dve.wait_ge(s_winT, T + 1)
                dve.tensor_copy(idx[:, slot, :], tables[:, 0:SLOTS]).then_inc(s_idx, 1)
                dve.tensor_scalar(place[:, slot, :], tables[:, SLOTS:2 * SLOTS],
                                  first_node[:, bass.ds(T, 1)], None, ALU.subtract).then_inc(s_place, 1)

            def one_hots(T, i, slot, piece, first=False, signal=s_onehot):
                dve.wait_ge(s_place, T + 1)
                if not first:
                    dve.wait_ge(s_seg, PAIRED * (T - 1))
                k0, k1 = ONEHOT_PIECES[piece]
                shape = [P, k1 - k0, TN]
                dve.tensor_tensor(onehot[:, i, k0:k1, :],
                                  iota_row[:, 0:TN].unsqueeze(1).to_broadcast(shape),
                                  place[:, slot, k0:k1].unsqueeze(2).to_broadcast(shape),
                                  ALU.is_equal).then_inc(signal, 1)

            window_tables(0, 0)

            dve.wait_ge(s_dst, 16)
            link(dve.tensor_copy(lastf[0:RP, :], dsti[:, :, ROW - 1]))
            shape = [RP, BLK, TILES]
            link(dve.tensor_tensor(below[0:RP, :, :], first_node[0:RP, 0:TILES].unsqueeze(1).to_broadcast(shape),
                                   lastf[0:RP, :].unsqueeze(2).to_broadcast(shape), ALU.is_gt))
            assert count[0] == PREP_BELOW
            one_hots(0, 0, 0, 0, True)
            dve.wait_ge(s_prep_pe, 1)
            link(dve.tensor_scalar(rowidx[0:TILES, :], tables[0:TILES, 0:1], float(BLK * RP - 1), None,
                                   ALU.min))
            assert count[0] == PREP_ROWIDX
            link(dve.tensor_copy(boundary[0:TILES, 0:1], rowidx[0:TILES, :]))
            one_hots(0, 0, 0, 1, True)
            dve.wait_ge(s_next, 16 * (BLK + 1))
            link(dve.tensor_tensor(falls.rearrange("p (b j) -> p b j", b=BLK), dsti[:, :, 0:ROW], dsti[:, :, 1:ROW + 1], ALU.subtract))
            link(dve.tensor_reduce(verdict[0:RP, 0:1], falls, AX.X, ALU.max))
            link(dve.tensor_scalar(verdict[0:RP, 1:2], verdict[0:RP, 0:1], 0.0, None, ALU.is_gt))
            one_hots(0, 0, 0, 2, True)
            dve.wait_ge(s_rowdst, 16)
            link(dve.tensor_scalar(rowcmp[0:TILES, :], rowdst[0:TILES, :], first_node_col[0:TILES, 0:1], None,
                                   ALU.is_lt))
            link(dve.tensor_reduce(boundary[0:TILES, 1:2], rowcmp[0:TILES, :], AX.X, ALU.add))
            link(dve.scalar_tensor_tensor(out=boundary[0:TILES, 2:3], in0=boundary[0:TILES, 0:1],
                                          scalar=float(ROW), in1=boundary[0:TILES, 1:2],
                                          op0=ALU.mult, op1=ALU.add))
            link(dve.tensor_scalar(boundary[0:TILES, 3:4], boundary[0:TILES, 2:3], float(E - WIN), None,
                                   ALU.min))
            assert count[0] == PREP_BOUNDARY
            cut_weights(0)
            dve.wait_ge(s_prep_pe, 2)
            dve.tensor_copy(start[0:1, 0:TILES], tables[0:1, 128:128 + TILES]).then_inc(s_start, 1)
            dve.tensor_copy(startf[:, :], tables[0:1, 128:128 + TILES]).then_inc(s_start, 1)
            dve.tensor_copy(runs[0:1, 0:TILES], tables[0:1, 64:64 + TILES]).then_inc(s_start, 1)
            dve.wait_ge(s_start, 3)
            link(dve.tensor_tensor(runlen[:, :], runs[:, 1:TILES + 1], startf[:, :], ALU.subtract))
            link(dve.tensor_reduce(verdict[0:1, 2:3], runlen[:, :], AX.X, ALU.max))
            link(dve.tensor_scalar(verdict[0:1, 3:4], verdict[0:1, 2:3], float(WIN), tables[0:1, 192:193],
                                   ALU.is_gt, ALU.add))
            dve.tensor_scalar(flag[:, :], verdict[0:1, 3:4], 0.5, None, ALU.is_gt).then_inc(s_flag, 1)
            dve.wait_ge(s_small, 32)
            dve.tensor_scalar(onepe[:, 1:2], onepe[:, 0:1], 1.0, None, ALU.add).then_inc(s_const, 1)
            dve.wait_ge(s_const, CONSTS)
            cut_weights(1)
            dve.wait_ge(s_flag, 1)

            general = dve.value_load(flag[0:1, 0:1], min_val=0, max_val=1)
            with dve.If(general > 0):
                dve.wait_ge(g_step, 1)
                dve.tensor_scalar(lower, iota_row[0:GT, 0:GT], iota_col[0:GT, 0:1], None,
                                  ALU.is_lt).then_inc(g_dve, 1)
                with dve.Fori(0, GTILES) as t:
                    dve.wait_ge(g_edge, 32 * t + 32)
                    dve.wait_ge(g_dve, 7 * t + 1)
                    dve.tensor_copy(boundary[0:GT, 0:1], rowdst[0:GT, 0:1]).then_inc(g_dve, 1)
                    dve.wait_ge(g_dve, 7 * t + 2)
                    dve.tensor_copy(copies, boundary[0:GT, 0:1].to_broadcast([GT, GT])).then_inc(g_dve, 1)
                    dve.wait_ge(g_pe, 2 * t + 1)
                    dve.wait_ge(g_dve, 7 * t + 3)
                    dve.tensor_scalar(same, acc[0][0:GT, 0:GT], boundary[0:GT, 0:1], None,
                                      ALU.is_equal).then_inc(g_dve, 1)
                    dve.wait_ge(g_dve, 7 * t + 4)
                    dve.tensor_tensor(earlier, same, lower, ALU.mult).then_inc(g_dve, 1)
                    dve.wait_ge(g_dve, 7 * t + 5)
                    dve.tensor_reduce(boundary[0:GT, 1:2], earlier, AX.X, ALU.add).then_inc(g_dve, 1)
                    dve.wait_ge(g_dve, 7 * t + 6)
                    dve.scalar_tensor_tensor(out=rowdst[0:GT, 1:2], in0=boundary[0:GT, 1:2], scalar=FAR,
                                             in1=boundary[0:GT, 0:1], op0=ALU.mult,
                                             op1=ALU.add).then_inc(g_dve, 1)
                    dve.wait_ge(g_pe, 2 * t + 2)
                    dve.wait_ge(g_got, 32 * t + 32)
                    dve.wait_ge(g_dve, 7 * t + 7)
                    dve.tensor_tensor(raw[0:GT, 2, :], acc[1][0:GT, :], raw[0:GT, 1, :],
                                      ALU.add).then_inc(g_dve, 1)
                dve.wait_ge(g_win, 32)
                dve.tensor_copy(winf[0:SLOTS, :, :], win[0:SLOTS, 0, :, :]).then_inc(g_winf, 1)
                dve.wait_ge(g_winT, 1)
                dve.tensor_copy(idx[:, 0, :], tables[:, 0:SLOTS]).then_inc(g_tab, 1)
                dve.tensor_scalar(place[:, 0, :], tables[:, SLOTS:2 * SLOTS], first_node[:, 0:1], None,
                                  ALU.subtract).then_inc(g_tab, 1)
                dve.wait_ge(g_tab, 2)
                for piece in range(3):
                    one_hots(0, 0, 0, piece, True, g_onehot)
                dve.wait_ge(g_onehot, 3)
                dve.wait_ge(g_again, 16 * SLOTS)
            dve.memset(startf[0:1, 0:1], 0.0).then_inc(s_go, 1)

            def make_rst(T, i, slot, lap, first):
                dve.wait_ge(s_seg, PAIRED * (T + 1))
                dve.wait_ge(s_x[slot], 32 * lap + 32)
                if type(T) is int and T == 0:
                    dve.wait_ge(s_wlo, ROOM.index(2) + 1)
                if not first:
                    dve.wait_ge(s_turn, T - 1)
                dve.scalar_tensor_tensor(out=rst[0:TN, i, :], in0=xt[0:TN, slot, :], scalar=onepe[0:TN, 1:2],
                                         in1=acc[i][0:TN, :], op0=ALU.mult, op1=ALU.add).then_inc(s_rst, 1)

            def rst_lo(T, i, half):
                dve.wait_ge(s_rhi, T + 1)
                cols = slice(i * TN, (i + 1) * TN)
                dve.tensor_tensor(rstT[1][:, half, :, cols], turned[:, :, 0:TN],
                                  rstT[0][:, half, :, cols].bitcast(F32), ALU.subtract).then_inc(s_rlo, 1)

            def h_lo(m, jp):
                dve.wait_ge(s_hhi, PAIRS * m + jp + 1)
                dve.tensor_tensor(hT[1][:, 2 * jp:2 * jp + 2, :], hfull[:, jp % 2, :, :],
                                  hT[0][:, 2 * jp:2 * jp + 2, :].bitcast(F32), ALU.subtract).then_inc(s_hlo, 1)

            def double_x(F, slot):
                dve.wait_ge(s_rst, F + 1)
                if type(F) is int and F == 0:
                    dve.wait_ge(s_b2, 16)
                dve.scalar_tensor_tensor(out=xt[0:TN, slot, :], in0=xt[0:TN, slot, :], scalar=2.0,
                                         in1=b2b[0:TN, :], op0=ALU.mult, op1=ALU.add).then_inc(s_double, 1)

            def residuals(F, f, slot, stores):
                dve.wait_ge(s_double, F + 1)
                if stores is not None:
                    dve.wait_ge(s_store[f], stores)
                wait_apart(dve, s_y, F + 1)
                dve.tensor_tensor(z[0:TN, f, :], xt[0:TN, slot, :], y[f][0:TN, :], ALU.add).then_inc(s_z, 1)

            def take_moments(F, f):
                dve.wait_ge(s_z, F + 1)
                dve.bn_stats(moments[0:TN, f, :], z[0:TN, f, :]).then_inc(s_mom, 1)
                wait_apart(dve, s_mom, F + 1)
                dve.bn_aggr(meanvar[0:TN, f, :], moments[0:TN, f, :]).then_inc(s_mv, 1)

            def scale_shift(F, f):
                dve.wait_ge(s_std, F + 1)
                dve.reciprocal(rstd[0:TN, f:f + 1], std[0:TN, f:f + 1]).then_inc(s_rstd, 1)
                dve.wait_ge(s_rstd, F + 1)
                dve.scalar_tensor_tensor(out=shift[0:TN, f:f + 1], in0=meanvar[0:TN, f, 0:1], scalar=-1.0,
                                         in1=rstd[0:TN, f:f + 1], op0=ALU.mult,
                                         op1=ALU.mult).then_inc(s_shift, 1)

            def group(g, res, lap):
                T0 = 2 * g
                static = type(g) is int
                half = 0 if res == 0 else 1
                for p in range(STEPS):
                    i, kp = p // PAIRED, p % PAIRED
                    T = T0 + i
                    n = min(2, SLOTS - 2 * kp)
                    if not (static and T == 0 and kp < WHOLE):
                        dve.wait_ge(s_mhi, PAIRED * T + kp + 1 - WHOLE)
                        dve.tensor_tensor(msg[1][:, p % RING, 0:n, :], raw[:, 2 * kp:2 * kp + n, :],
                                          msg[0][:, p % RING, 0:n, :].bitcast(F32),
                                          ALU.subtract).then_inc(s_mlo, 1)
                    if static and p + STEPS * g in CUT_STEP:
                        cut_weights(2 + CUT_STEP.index(p + STEPS * g))
                    if static and T == 0:
                        for w in range(2):
                            if kp == FIRST_TABLES[w]:
                                window_tables(1 + w, 1 + w)
                    elif kp == AT_TABLES:
                        window_tables(T + 2, (res + i + 2) % 4)
                    for piece in range(3):
                        if kp == (FIRST_ONEHOT if static and T == 0 else AT_ONEHOT)[piece]:
                            one_hots(T + 1, 1 - i, (res + i + 1) % 4, piece, static and T < 1)
                    if kp == AT_RST and not (static and T == 0):
                        make_rst(T - 1, 1 - i, (res + i - 1) % 4, lap + (res + i - 1) // 4, static and T < 3)
                    if kp == AT_RST_LO and not (static and T == 0):
                        rst_lo(T - 1, 1 - i, half if i else 1 - half)
                    for jp in range(PAIRS):
                        if p == HLO_STEP[jp] and not (static and g < 1):
                            h_lo(g - 1, jp)
                        if p == HLO_STEP[jp] - STEPS and not (static and g < 2):
                            h_lo(g - 2, jp)
                    if static and g < 2:
                        continue
                    for f in range(2):
                        F = T0 - 4 + f
                        if p == DOUBLE_STEP[f]:
                            double_x(F, (res + f) % 4)
                        if p == Z_STEP[f]:
                            residuals(F, f, (res + f) % 4, None if static and g < 3 else 32 * (g - 2))
                        if p == MOM_STEP[f]:
                            take_moments(F, f)
                        if p == RSTD_STEP[f]:
                            scale_shift(F, f)

            pair = run_groups(group)
            with dve.Fori(1, GROUPS // 2) as it:
                pair(it)
            last = GROUPS - 1
            for jp in range(PAIRS):
                if HLO_STEP[jp] >= STEPS:
                    h_lo(last - 1, jp)
            make_rst(TILES - 1, 1, (TILES - 1) % 4, (TILES - 1) // 4, False)
            rst_lo(TILES - 1, 1, last % 2)
            for F in range(TILES - 4, TILES):
                if F < TILES - 2:
                    double_x(F, F % 4)
                if F == TILES - 2:
                    for f in range(2):
                        double_x(F + f, (F + f) % 4)
                    for jp in range(PAIRS):
                        h_lo(last, jp)
                residuals(F, F % 2, F % 4, 32 * (F // 2))
                take_moments(F, F % 2)
                scale_shift(F, F % 2)

        @block.tensor
        def _(pe):
            def window_T(T, first=False):
                if first:
                    pe.wait_ge(s_winf, 1)
                else:
                    wait_apart(pe, s_place, T)
                    wait_apart(pe, s_winf, T + 1)
                for s in range(2):
                    mm = pe.transpose(tables[:, s * SLOTS:(s + 1) * SLOTS], winf[0:SLOTS, s, :],
                                      ident[0:SLOTS, 0:SLOTS])
                mm.then_inc(s_winT, 1)

            pe.wait_ge(s_const, CONSTS - 1)
            window_T(0, True)

            pe.wait_ge(s_prep, PREP_BELOW)
            pe.wait_ge(s_place, 1)
            for b in range(BLK):
                mm = pe.matmul(tables[0:TILES, 0:1], below[0:RP, b, :], ones[0:RP, :],
                               start=(b == 0), stop=(b == BLK - 1))
            mm.then_inc(s_prep_pe, 1)
            pe.wait_ge(s_prep, PREP_BOUNDARY)
            pe.matmul(tables[0:1, 64:64 + TILES], boundary[0:TILES, 2:3], ident[0:TILES, 0:TILES],
                      start=True, stop=True)
            pe.matmul(tables[0:1, 128:128 + TILES], boundary[0:TILES, 3:4], ident[0:TILES, 0:TILES],
                      start=True, stop=True)
            pe.matmul(tables[0:1, 192:193], verdict[0:RP, 1:2], ones[0:RP, :],
                      start=True, stop=True).then_inc(s_prep_pe, 1)

            pe.wait_ge(s_flag, 1)
            general = pe.value_load(flag[0:1, 0:1], min_val=0, max_val=1)
            with pe.If(general > 0):
                with pe.Fori(0, GTILES) as t:
                    pe.wait_ge(g_dve, 7 * t + 3)
                    pe.matmul(acc[0][0:GT, 0:GT], copies, ident[0:GT, 0:GT],
                              start=True, stop=True).then_inc(g_pe, 1)
                    pe.wait_ge(g_dve, 7 * t + 4)
                    pe.wait_ge(g_got, 32 * t + 32)
                    pe.matmul(acc[1][0:GT, :], same, raw[0:GT, 0, :],
                              start=True, stop=True).then_inc(g_pe, 1)
                pe.wait_ge(g_winf, 1)
                for s in range(2):
                    mm = pe.transpose(tables[:, s * SLOTS:(s + 1) * SLOTS], winf[0:SLOTS, s, :],
                                      ident[0:SLOTS, 0:SLOTS])
                mm.then_inc(g_winT, 1)

            def rst_T(T, i, first):
                pe.wait_ge(s_rst, T + 1)
                if not first:
                    pe.wait_ge(s_rlo, T)
                for c in range(TC):
                    mm = pe.transpose(turned[:, c, 0:TN], rst[0:TN, i, c * P:(c + 1) * P],
                                      ident[0:TN, 0:TN])
                mm.then_inc(s_turn, 1)

            def layer1(m, half, first):
                for n in range(L1_PRODUCTS):
                    j, c, term = n // (TC * 3), n // 3 % TC, n % 3
                    jp, jj = j // 2, j % 2
                    if n == 0:
                        pe.wait_ge(s_rlo, 2 * m + 2)
                        if first:
                            pe.wait_ge(s_wlo, TC)
                    if c == 0 and term == 0 and jj == 0 and not (first and jp < 2):
                        pe.wait_ge(s_relu, HC * m + 2 * jp - 2)
                    a, b = ((0, 0), (0, 1), (1, 0))[term]
                    mm = pe.matmul(hp[jp % 2][:, jj, :], w1[a][:, c, j * P:(j + 1) * P], rstT[b][:, half, c, :],
                                   start=(c == 0 and term == 0), stop=(c == TC - 1 and term == 2))
                    if c == TC - 1 and term == 2:
                        mm.then_inc(s_mm1, 1)
                    yield

            def layer2(m, first, done=0):
                for n in range(done, L2_PRODUCTS):
                    f, j, term = n // (HC * 3), n // 3 % HC, n % 3
                    if j == 0 and term == 0 and not first:
                        pe.wait_ge(s_z, 2 * m + f - 1)
                    if f == 0 and j % 2 == 0 and term == 0:
                        pe.wait_ge(s_hlo, PAIRS * m + j // 2 + 1)
                    if n == 0 and first:
                        pe.wait_ge(s_wlo, WPIECES)
                    a, b = ((0, 0), (0, 1), (1, 0))[term]
                    mm = pe.matmul(y[f][0:TN, :], hT[a][:, j, f * TN:(f + 1) * TN], w2[b][:, j, :],
                                   start=(j == 0 and term == 0), stop=(j == HC - 1 and term == 2))
                    if j == HC - 1 and term == 2:
                        mm.then_inc(s_y, 1)
                    yield

            def share(products, steps, q):
                return products * (q + 1) // steps - products * q // steps

            def take(work, n):
                for _ in range(n):
                    next(work, None)

            def group(g, res, lap):
                T0 = 2 * g
                static = type(g) is int
                half = 0 if res == 0 else 1
                one = layer1(g - 1, 1 - half, static and g < 2)
                two = layer2(g - 1, static and g < 2)
                two_before = layer2(g - 2, static and g < 3, L2_PRODUCTS * (STEPS - L2_STEP) // L2_STEPS)
                for p in range(STEPS):
                    i, kp = p // PAIRED, p % PAIRED
                    T = T0 + i
                    for piece in range(3):
                        if 2 * kp == ONEHOT_PIECES[piece][0]:
                            pe.wait_ge(s_onehot, 3 * T + piece + 1)
                    if kp == 0 and not (static and T < 2):
                        pe.wait_ge(s_rst, T - 1)
                    whole = static and T == 0 and kp < WHOLE
                    if whole:
                        pe.wait_ge(s_gather[kp], 16 * min(2, SLOTS - 2 * kp))
                    else:
                        pe.wait_ge(s_mlo, PAIRED * T + kp + 1 - WHOLE)
                    for k in range(2 * kp, min(2 * kp + 2, SLOTS)):
                        if whole:
                            mm = pe.matmul(acc[0][0:TN, :], onehot[:, 0, k, :].bitcast(F32), raw[:, k, :],
                                           start=(k == 0), stop=False)
                            continue
                        for s in range(2):
                            mm = pe.matmul(acc[i][0:TN, :], onehot[:, i, k, :], msg[s][:, p % RING, k % 2, :],
                                           start=(k == 0 and s == 0), stop=(k == SLOTS - 1 and s == 1))
                    mm.then_inc(s_seg, 1)
                    if static and T == 0:
                        for w in range(2):
                            if kp == FIRST_WINDOW_T[w]:
                                window_T(1 + w)
                    elif kp == AT_WINDOW_T:
                        window_T(T + 2)
                    if kp == AT_RST_T and not (static and T == 0):
                        rst_T(T - 1, 1 - i, static and T == 1)
                    if 0 <= p - L1_STEP < L1_STEPS and not (static and g < 1):
                        take(one, share(L1_PRODUCTS, L1_STEPS, p - L1_STEP))
                    if p >= L2_STEP and not (static and g < 1):
                        take(two, share(L2_PRODUCTS, L2_STEPS, p - L2_STEP))
                    if p + STEPS - L2_STEP < L2_STEPS and not (static and g < 2):
                        take(two_before, share(L2_PRODUCTS, L2_STEPS, p + STEPS - L2_STEP))

            pe.wait_ge(s_go, 1)
            pair = run_groups(group)
            with pe.Fori(1, GROUPS // 2) as it:
                pair(it)
            last = GROUPS - 1
            two = layer2(last - 1, False, L2_PRODUCTS * (STEPS - L2_STEP) // L2_STEPS)
            take(two, HC)
            rst_T(TILES - 1, 1, False)
            take(two, L2_PRODUCTS)
            take(layer1(last, last % 2, False), L1_PRODUCTS)
            take(layer2(last, False), L2_PRODUCTS)


PREP_BELOW = 2
PREP_ROWIDX = PREP_BELOW + 1
PREP_BOUNDARY = PREP_ROWIDX + 8
CONSTS = 6

_INS = ['x', 'src', 'dst', 'L0_gnn_W1', 'L0_gnn_b1', 'L0_gnn_W2', 'L0_gnn_b2', 'L0_gnn_eps']


def kernel(**inputs):
    import numpy as _np
    import concourse.bacc as _bacc
    from concourse.bass_utils import run_bass_kernel_spmd as _run

    nc = _bacc.Bacc("TRN2", target_bir_lowering=False, num_devices=1)
    arrays, args = {}, []
    for name in _INS:
        a = _np.ascontiguousarray(inputs[name])
        arrays[f"in_{name}_dram"] = a
        args.append(nc.dram_tensor(f"in_{name}_dram", a.shape, mybir.dt.from_np(a.dtype), kind="ExternalInput").ap())
    args.append(nc.dram_tensor("out_dram", (N, D), F32, kind="ExternalOutput").ap())
    build(nc, *args)
    r = _run(nc, [arrays], core_ids=[0])
    return r.results[0]["out_dram"]
```
